# Optimizing a Trainium2 kernel written in Bass

```python
import numpy as np
import jax
import jax.numpy as jnp

def _softmax(x, axis=-1):
    return jax.nn.softmax(x, axis=axis)

def _gelu(x):
    return jax.nn.gelu(x, approximate=True)

def _silu(x):
    return jax.nn.silu(x)

def _sigmoid(x):
    return jax.nn.sigmoid(x)

def _layernorm(x, axis=-1, eps=1e-05):
    m = jnp.mean(x, axis=axis, keepdims=True)
    v = jnp.var(x, axis=axis, keepdims=True)
    return (x - m) / jnp.sqrt(v + eps)

def _scatter_add(tgt, idx, src, axis=0):
    return tgt.at[idx].add(src)

def _segment_sum(src, seg, n):
    return jax.ops.segment_sum(src, seg, n)
kernel_name = 'mk_seq_preln_d1_jaxref_r8_edcba7'

def setup_inputs(seed: int=0):
    np.random.seed(seed)
    _w = jnp.asarray

    def _L0_attn_setup():
        import jax, jax.numpy as jnp
        import numpy as np
        import math
        D_MODEL = 128
        N_HEADS = 16
        BASE = 1250
        B, T = (8, 128)

        def hope_bias(pos_independent, T, d_model, n_heads, base):
            dim = d_model // 2
            pos = np.arange(dim, dtype=np.float64)
            freqs_np = 1.0 / base ** (pos / dim)
            active = int(np.sum(freqs_np * 2 * math.pi * T >= 1.0))
            active = min(active, dim - d_model // 4)
            freqs = jnp.asarray(freqs_np[:active], dtype=jnp.float32)
            d = jnp.arange(-(T - 1), T, dtype=jnp.float32)
            theta = d[:, None] * freqs[None, :]
            pv_high = jnp.cos(theta) + jnp.sin(theta)
            latter = dim - active
            pv_const = pos_independent[:latter].sum(axis=-1)
            pv = jnp.concatenate([pv_high, jnp.broadcast_to(pv_const[None, :], (2 * T - 1, latter))], axis=1)
            pairs_per_head = dim // n_heads
            per_head = pv.reshape(2 * T - 1, n_heads, pairs_per_head).sum(axis=-1)
            idx = jnp.arange(T)[:, None] - jnp.arange(T)[None, :] + (T - 1)
            return per_head[idx]
        key = jax.random.key(seed)
        ks = jax.random.split(key, 6)
        d = D_MODEL
        return {'x': jax.random.normal(ks[0], (B, T, d), dtype=jnp.float32), 'w_qkv': jax.random.normal(ks[1], (3 * d, d), dtype=jnp.float32) * 0.02, 'b_qkv': jnp.zeros((3 * d,), dtype=jnp.float32), 'w_proj': jax.random.normal(ks[2], (d, d), dtype=jnp.float32) * 0.02, 'b_proj': jnp.zeros((d,), dtype=jnp.float32), 'pos_independent': jax.random.normal(ks[3], (d // 4, 2), dtype=jnp.float32)}
    _L0_attn_in = _L0_attn_setup()

    def _L0_ffn_setup():
        import jax, jax.numpy as jnp
        import numpy as np
        DIM = 128
        DEPTH = 6
        HEADS = 16
        DIM_HEAD = 64
        WINDOW = 32
        INNER = HEADS * DIM_HEAD
        DIM_INNER = int(DIM * 4 * 2 / 3)
        QK_SCALE = 8.0

        def shift_tokens(t):
            a, s = jnp.split(t, 2, -1)
            s = jnp.pad(s, ((0, 0), (1, 0), (0, 0)))[:, :-1]
            return jnp.concatenate([a, s], -1)

        def l2norm(t):
            return t / jnp.maximum(jnp.linalg.norm(t, axis=-1, keepdims=True), 1e-12)

        def rotate_half(x):
            x1, x2 = jnp.split(x, 2, -1)
            return jnp.concatenate([-x2, x1], -1)

        def rotary_tables(n):
            half = jnp.arange(0, DIM_HEAD, 2, dtype=jnp.float32)
            inv_freq = 1.0 / 10000.0 ** (half / DIM_HEAD)
            t = jnp.arange(n, dtype=jnp.float32)
            freqs = t[:, None] * inv_freq[None, :]
            freqs = jnp.concatenate([freqs, freqs], -1)
            base_scale = (half + 0.4 * DIM_HEAD) / (1.4 * DIM_HEAD)
            power = (t - n // 2) / (WINDOW // 2)
            scale = base_scale[None, :] ** power[:, None]
            scale = jnp.concatenate([scale, scale], -1)
            return (freqs, scale)

        def local_attention(q, k, v):
            b, h, n, d = q.shape
            w = WINDOW
            nw = n // w
            bq = q.reshape(b, h, nw, w, d)
            bk = k.reshape(b, h, nw, w, d)
            bv = v.reshape(b, h, nw, w, d)

            def look(t):
                p = jnp.pad(t, ((0, 0), (0, 0), (1, 0), (0, 0), (0, 0)))
                return jnp.concatenate([p[:, :, :nw], p[:, :, 1:]], axis=3)
            bk2, bv2 = (look(bk), look(bv))
            seq = jnp.arange(n).reshape(nw, w)
            seq_p = jnp.pad(seq, ((1, 0), (0, 0)), constant_values=-1)
            jt = jnp.concatenate([seq_p[:nw], seq_p[1:]], axis=1)
            it = seq[:, :, None]
            jb = jt[:, None, :]
            mask = (it < jb) | (it > jb + w) | (jb == -1)
            sim = jnp.einsum('bhwie,bhwje->bhwij', bq, bk2) * QK_SCALE
            sim = jnp.where(mask, -jnp.finfo(sim.dtype).max, sim)
            attn = jax.nn.softmax(sim, -1)
            out = jnp.einsum('bhwij,bhwje->bhwie', attn, bv2)
            return out.reshape(b, h, n, d)

        def attn_layer(x, Wqkv, qs, ksc, Wo):
            b, n, _ = x.shape
            qkv = x @ Wqkv
            q, k, v = jnp.split(qkv, 3, -1)
            sh = lambda t: t.reshape(b, n, HEADS, DIM_HEAD).transpose(0, 2, 1, 3)
            q, k, v = (sh(q), sh(k), sh(v))
            q = l2norm(q) * qs
            k = l2norm(k) * ksc
            freqs, scale = rotary_tables(n)
            cos, sin = (jnp.cos(freqs), jnp.sin(freqs))
            q = q * cos * scale + rotate_half(q) * sin * scale
            inv = 1.0 / scale
            k = k * cos * inv + rotate_half(k) * sin * inv
            out = local_attention(q, k, v)
            out = out.transpose(0, 2, 1, 3).reshape(b, n, INNER)
            return out @ Wo

        def ffn_layer(x, g, bln, W1, b1, W2, b2):
            mu = x.mean(-1, keepdims=True)
            var = ((x - mu) ** 2).mean(-1, keepdims=True)
            xn = (x - mu) / jnp.sqrt(var + 1e-05) * g + bln
            hg = xn @ W1 + b1
            a, gate = jnp.split(hg, 2, -1)
            return a * jax.nn.gelu(gate, approximate=False) @ W2 + b2
        key = jax.random.key(seed)
        ks = jax.random.split(key, 8)
        B, N = (2, 256)
        init = lambda k, shape: jax.random.normal(k, shape, jnp.float32) * 0.02
        return {'x': jax.random.normal(ks[0], (B, N, DIM), jnp.float32), 'Wqkv': init(ks[1], (DEPTH, DIM, 3 * INNER)), 'q_scale': jnp.ones((DEPTH, DIM_HEAD), jnp.float32), 'k_scale': jnp.ones((DEPTH, DIM_HEAD), jnp.float32), 'Wo': init(ks[2], (DEPTH, INNER, DIM)), 'ln_g': jnp.ones((DEPTH, DIM), jnp.float32), 'ln_b': jnp.zeros((DEPTH, DIM), jnp.float32), 'W1': init(ks[3], (DEPTH, DIM, 2 * DIM_INNER)), 'b1': jnp.zeros((DEPTH, 2 * DIM_INNER), jnp.float32), 'W2': init(ks[4], (DEPTH, DIM_INNER, DIM)), 'b2': jnp.zeros((DEPTH, DIM), jnp.float32)}
    _L0_ffn_in = _L0_ffn_setup()
    _d = {'L0_attn_x': _L0_attn_in['x'], 'L0_attn_w_qkv': _L0_attn_in['w_qkv'], 'L0_attn_b_qkv': _L0_attn_in['b_qkv'], 'L0_attn_w_proj': _L0_attn_in['w_proj'], 'L0_attn_b_proj': _L0_attn_in['b_proj'], 'L0_attn_pos_independent': _L0_attn_in['pos_independent'], 'L0_ffn_Wqkv': _L0_ffn_in['Wqkv'], 'L0_ffn_q_scale': _L0_ffn_in['q_scale'], 'L0_ffn_k_scale': _L0_ffn_in['k_scale'], 'L0_ffn_Wo': _L0_ffn_in['Wo'], 'L0_ffn_ln_g': _L0_ffn_in['ln_g'], 'L0_ffn_ln_b': _L0_ffn_in['ln_b'], 'L0_ffn_W1': _L0_ffn_in['W1'], 'L0_ffn_b1': _L0_ffn_in['b1'], 'L0_ffn_W2': _L0_ffn_in['W2'], 'L0_ffn_b2': _L0_ffn_in['b2']}
    _x0 = _d['L0_attn_x']
    _d['L0_attn_x'] = jax.random.normal(jax.random.fold_in(jax.random.key(seed), 1), (16, 256, 128), dtype=_x0.dtype)
    del _x0
    return _d

def reference(L0_attn_x, L0_attn_w_qkv, L0_attn_b_qkv, L0_attn_w_proj, L0_attn_b_proj, L0_attn_pos_independent, L0_ffn_Wqkv, L0_ffn_q_scale, L0_ffn_k_scale, L0_ffn_Wo, L0_ffn_ln_g, L0_ffn_ln_b, L0_ffn_W1, L0_ffn_b1, L0_ffn_W2, L0_ffn_b2):

    def _L0_attn_ref(x, w_qkv, b_qkv, w_proj, b_proj, pos_independent):
        import jax, jax.numpy as jnp
        import numpy as np
        import math
        D_MODEL = 128
        N_HEADS = 16
        BASE = 1250
        B, T = (8, 128)

        def hope_bias(pos_independent, T, d_model, n_heads, base):
            dim = d_model // 2
            pos = np.arange(dim, dtype=np.float64)
            freqs_np = 1.0 / base ** (pos / dim)
            active = int(np.sum(freqs_np * 2 * math.pi * T >= 1.0))
            active = min(active, dim - d_model // 4)
            freqs = jnp.asarray(freqs_np[:active], dtype=jnp.float32)
            d = jnp.arange(-(T - 1), T, dtype=jnp.float32)
            theta = d[:, None] * freqs[None, :]
            pv_high = jnp.cos(theta) + jnp.sin(theta)
            latter = dim - active
            pv_const = pos_independent[:latter].sum(axis=-1)
            pv = jnp.concatenate([pv_high, jnp.broadcast_to(pv_const[None, :], (2 * T - 1, latter))], axis=1)
            pairs_per_head = dim // n_heads
            per_head = pv.reshape(2 * T - 1, n_heads, pairs_per_head).sum(axis=-1)
            idx = jnp.arange(T)[:, None] - jnp.arange(T)[None, :] + (T - 1)
            return per_head[idx]
        Bm, Tm, C = x.shape
        H = N_HEADS
        hd = C // H
        qkv = x @ w_qkv.T + b_qkv
        qkv = qkv.reshape(Bm, Tm, 3, H, hd).transpose(2, 0, 3, 1, 4)
        q, k, v = (qkv[0], qkv[1], qkv[2])
        att = jnp.einsum('bhqd,bhkd->bhqk', q, k) / jnp.sqrt(jnp.float32(hd))
        bias = hope_bias(pos_independent, Tm, C, H, BASE)
        att = att + bias.transpose(2, 0, 1)[None]
        causal = jnp.tril(jnp.ones((Tm, Tm), dtype=bool))
        att = jnp.where(causal[None, None], att, -jnp.inf)
        att = jax.nn.softmax(att, axis=-1)
        out = jnp.einsum('bhqk,bhkd->bhqd', att, v)
        out = out.transpose(0, 2, 1, 3).reshape(Bm, Tm, C)
        return out @ w_proj.T + b_proj

    def _L0_ffn_ref(x, Wqkv, q_scale, k_scale, Wo, ln_g, ln_b, W1, b1, W2, b2):
        import jax, jax.numpy as jnp
        import numpy as np
        DIM = 128
        DEPTH = 6
        HEADS = 16
        DIM_HEAD = 64
        WINDOW = 32
        INNER = HEADS * DIM_HEAD
        DIM_INNER = int(DIM * 4 * 2 / 3)
        QK_SCALE = 8.0

        def shift_tokens(t):
            a, s = jnp.split(t, 2, -1)
            s = jnp.pad(s, ((0, 0), (1, 0), (0, 0)))[:, :-1]
            return jnp.concatenate([a, s], -1)

        def l2norm(t):
            return t / jnp.maximum(jnp.linalg.norm(t, axis=-1, keepdims=True), 1e-12)

        def rotate_half(x):
            x1, x2 = jnp.split(x, 2, -1)
            return jnp.concatenate([-x2, x1], -1)

        def rotary_tables(n):
            half = jnp.arange(0, DIM_HEAD, 2, dtype=jnp.float32)
            inv_freq = 1.0 / 10000.0 ** (half / DIM_HEAD)
            t = jnp.arange(n, dtype=jnp.float32)
            freqs = t[:, None] * inv_freq[None, :]
            freqs = jnp.concatenate([freqs, freqs], -1)
            base_scale = (half + 0.4 * DIM_HEAD) / (1.4 * DIM_HEAD)
            power = (t - n // 2) / (WINDOW // 2)
            scale = base_scale[None, :] ** power[:, None]
            scale = jnp.concatenate([scale, scale], -1)
            return (freqs, scale)

        def local_attention(q, k, v):
            b, h, n, d = q.shape
            w = WINDOW
            nw = n // w
            bq = q.reshape(b, h, nw, w, d)
            bk = k.reshape(b, h, nw, w, d)
            bv = v.reshape(b, h, nw, w, d)

            def look(t):
                p = jnp.pad(t, ((0, 0), (0, 0), (1, 0), (0, 0), (0, 0)))
                return jnp.concatenate([p[:, :, :nw], p[:, :, 1:]], axis=3)
            bk2, bv2 = (look(bk), look(bv))
            seq = jnp.arange(n).reshape(nw, w)
            seq_p = jnp.pad(seq, ((1, 0), (0, 0)), constant_values=-1)
            jt = jnp.concatenate([seq_p[:nw], seq_p[1:]], axis=1)
            it = seq[:, :, None]
            jb = jt[:, None, :]
            mask = (it < jb) | (it > jb + w) | (jb == -1)
            sim = jnp.einsum('bhwie,bhwje->bhwij', bq, bk2) * QK_SCALE
            sim = jnp.where(mask, -jnp.finfo(sim.dtype).max, sim)
            attn = jax.nn.softmax(sim, -1)
            out = jnp.einsum('bhwij,bhwje->bhwie', attn, bv2)
            return out.reshape(b, h, n, d)

        def attn_layer(x, Wqkv, qs, ksc, Wo):
            b, n, _ = x.shape
            qkv = x @ Wqkv
            q, k, v = jnp.split(qkv, 3, -1)
            sh = lambda t: t.reshape(b, n, HEADS, DIM_HEAD).transpose(0, 2, 1, 3)
            q, k, v = (sh(q), sh(k), sh(v))
            q = l2norm(q) * qs
            k = l2norm(k) * ksc
            freqs, scale = rotary_tables(n)
            cos, sin = (jnp.cos(freqs), jnp.sin(freqs))
            q = q * cos * scale + rotate_half(q) * sin * scale
            inv = 1.0 / scale
            k = k * cos * inv + rotate_half(k) * sin * inv
            out = local_attention(q, k, v)
            out = out.transpose(0, 2, 1, 3).reshape(b, n, INNER)
            return out @ Wo

        def ffn_layer(x, g, bln, W1, b1, W2, b2):
            mu = x.mean(-1, keepdims=True)
            var = ((x - mu) ** 2).mean(-1, keepdims=True)
            xn = (x - mu) / jnp.sqrt(var + 1e-05) * g + bln
            hg = xn @ W1 + b1
            a, gate = jnp.split(hg, 2, -1)
            return a * jax.nn.gelu(gate, approximate=False) @ W2 + b2
        for i in range(DEPTH):
            x = attn_layer(shift_tokens(x), Wqkv[i], q_scale[i], k_scale[i], Wo[i]) + x
            x = ffn_layer(shift_tokens(x), ln_g[i], ln_b[i], W1[i], b1[i], W2[i], b2[i]) + x
        return x
    x = L0_attn_x
    x = x + _L0_attn_ref(_layernorm(x, axis=-1), L0_attn_w_qkv, L0_attn_b_qkv, L0_attn_w_proj, L0_attn_b_proj, L0_attn_pos_independent)
    x = x + _L0_ffn_ref(_layernorm(x, axis=-1), L0_ffn_Wqkv, L0_ffn_q_scale, L0_ffn_k_scale, L0_ffn_Wo, L0_ffn_ln_g, L0_ffn_ln_b, L0_ffn_W1, L0_ffn_b1, L0_ffn_W2, L0_ffn_b2)
    return x

_drawn_inputs = setup_inputs


def setup_inputs(seed=0):
    import zlib

    import numpy as np

    out = dict(_drawn_inputs(seed))
    spreads = {'L0_attn_b_qkv': (0.0, 0.312),
     'L0_attn_b_proj': (0.0, 0.1),
     'L0_ffn_q_scale': (1.0, 0.6),
     'L0_ffn_k_scale': (1.0, 0.6),
     'L0_ffn_ln_g': (1.0, 0.6),
     'L0_ffn_ln_b': (0.0, 0.8),
     'L0_ffn_b1': (0.0, 0.8),
     'L0_ffn_b2': (0.0, 0.1)}
    factors = {'L0_attn_w_qkv': 4.482,
     'L0_attn_pos_independent': 8.0,
     'L0_ffn_W1': 3.643,
     'L0_ffn_W2': 3.567}
    for name, (base, spread) in spreads.items():
        noise = np.random.default_rng([zlib.crc32(name.encode()), seed]).standard_normal(out[name].shape)
        drawn = base * np.exp(spread * noise) if base else spread * noise
        out[name] = jnp.asarray(drawn.astype(out[name].dtype))
    for name, factor in factors.items():
        out[name] = (out[name] * factor).astype(out[name].dtype)
    return out
```

```python
from contextlib import ExitStack

import concourse.bass as bass
import numpy as np
from concourse import mybir

F32 = mybir.dt.float32
BF16 = mybir.dt.bfloat16
ALU = mybir.AluOpType
ACT = mybir.ActivationFunctionType
AX = mybir.AxisListType.X

P = 128
B, T, D = 16, 256, 128
TQ = T // P
H = 16
HD0 = D // H
STRIP = 32
HPC0 = P // STRIP
NC0 = H // HPC0
HD = 64
HPC = P // HD
NCH = H // HPC
L = 6
WIN = 32
FI = 341
FC = 3
KB = P + WIN
S0W = 3 * P
EPS = 1e-5
MASKED = -1e30
NORM_GUARD = 1e-24

C_ID, C_CAUSAL, C_LOCAL, C_RQ, C_RK, C_BLK, C_ONE, C_POS = 0, 128, 512, 832, 1344, 1856, 1984, 1985
C_N = C_POS + 2 * P
A_Q, A_K, A_V, A_P, A_N = 0, 512, 1024, 1152, 1280
V_BQ, V_BK, V_BV, V_BP, V_POS, V_N = 0, 4, 8, 9, 10, 11
WCH = 5 * P
WA_N = NCH * WCH + 4
F_O, F_1, F_2, F_V = 0, 1024, 1792, 2176
F_G, F_B, F_B1, F_B2 = F_V, F_V + 1, F_V + 2, F_V + 8
WF_N = F_V + 9


def sequence_kernel(nc, x, consts, toeplitz, hope_w, hope_v, attn_w, ffn_w, out):
    with ExitStack() as ctx:
        def sb(name, shape, dt=F32):
            return ctx.enter_context(nc.sbuf_tensor(name, shape, dt))

        def sem(name):
            return ctx.enter_context(nc.semaphore(name))

        stream = sb("stream", [P, B * T])
        skip = sb("skip", [P, B * T])
        cst = sb("cst", [P, C_N])
        toep = sb("toep", [P, 8 * S0W])
        hw = sb("hw", [P, A_N])
        hv = sb("hv", [P, V_N])
        wa = sb("wa", [P, WA_N])
        wf = sb("wf", [P, WF_N])
        identb = sb("identb", [P, P], BF16)
        causalb = sb("causalb", [P, S0W], BF16)
        localb = sb("localb", [P, 2 * KB], BF16)
        mean_w = sb("mean_w", [P, P])
        eps = sb("eps", [P, 1])
        hbias = sb("hbias", [P, 8])
        qh = sb("qh", [P, NC0, T])
        kh = sb("kh", [P, NC0, T])
        v0 = sb("v0", [P, TQ, H, HD0 + 1])
        nmax0 = sb("nmax0", [P, H, TQ])
        prob0 = sb("prob0", [P, 2, S0W])
        pt0 = sb("pt0", [P, 2, S0W])
        rec0 = sb("rec0", [P, TQ * H])
        ao0 = sb("ao0", [P, TQ, D])
        aot0 = sb("aot0", [P, T])
        dev = sb("dev", [P, T])
        dsq = sb("dsq", [P, T])
        logv = sb("logv", [P, T])
        rstd = sb("rstd", [P, T])
        xn = sb("xn", [P, T])
        xs = sb("xs", [P, T])
        csq = sb("csq", [P, 2 * T])
        csk = sb("csk", [P, 2 * T])
        sqq = sb("sqq", [P, T])
        sqk = sb("sqk", [P, T])
        tq = sb("tq", [P, 2, 2 * T])
        tk = sb("tk", [P, 2, 2 * T])
        qr = sb("qr", [P, 2, T])
        ka = sb("ka", [P, 2, T])
        kr = sb("kr", [P, 2, T])
        ng = sb("ng", [P, T + 4])
        lg = sb("lg", [P, T + 4])
        rn = sb("rn", [P, 2, T + 4])
        nm = sb("nm", [P, 4])
        nb = sb("nb", [P, 2, 4])
        pa = sb("pa", [P, 2, HPC, P])
        pb = sb("pb", [P, 2, HPC, KB])
        pt = sb("pt", [P, 2, 4 * P])
        ptp = sb("ptp", [WIN, 2, HPC, WIN])
        vs = sb("vs", [P, 4, TQ, HPC, HD + 1])
        vp = sb("vp", [WIN, 4, HPC, HD + 1])
        rec = sb("rec", [P, 4])
        ao = sb("ao", [P, 2, TQ, P])
        aot = sb("aot", [P, NCH, T])
        xm = sb("xm", [P, T])
        xs2 = sb("xs2", [P, T])
        fval = sb("fval", [P, FC, T])
        fgate = sb("fgate", [P, FC, T])
        fact = sb("fact", [P, FC, T])
        fh = sb("fh", [P, FC, T])
        total = sb("total", [P, 4, T * B // 4])

        def bank(name):
            return ctx.enter_context(nc.psum_tensor(name, [P, 512], F32))

        PQ, PK, NV, S0, S1, TT, OO, FF = [bank(n) for n in ("PQ", "PK", "NV", "S0", "S1", "TT", "OO", "FF")]

        ident = cst[:, C_ID:C_ID + P]
        blk = cst[:, C_BLK:C_BLK + P]

        pos_done = sem("pos_done")
        mean_done = sem("mean_done")
        var_done = sem("var_done")
        q0_done = sem("q0_done")
        k0_done = sem("k0_done")
        v0_done = sem("v0_done")
        s0_done = sem("s0_done")
        t0_done = sem("t0_done")
        pv0_done = sem("pv0_done")
        aot0_done = sem("aot0_done")
        y0_done = sem("y0_done")
        q_done = sem("q_done")
        k_done = sem("k_done")
        v_done = sem("v_done")
        s_done = sem("s_done")
        n_done = sem("n_done")
        pv_done = sem("pv_done")
        t_done = sem("t_done")
        aot_done = sem("aot_done")
        y_done = sem("y_done")
        fmean_done = sem("fmean_done")
        fvar_done = sem("fvar_done")
        w1_done = sem("w1_done")
        w2_done = sem("w2_done")
        setup_ready = sem("setup_ready")
        casts_ready = sem("casts_ready")
        hbias_ready = sem("hbias_ready")
        dev_ready = sem("dev_ready")
        ln_ready = sem("ln_ready")
        k0_ready = sem("k0_ready")
        v0_ready = sem("v0_ready")
        max0_ready = sem("max0_ready")
        pt0_ready = sem("pt0_ready")
        rec0_ready = sem("rec0_ready")
        ao0_ready = sem("ao0_ready")
        x1_ready = sem("x1_ready")
        tables_ready = sem("tables_ready")
        xs_ready = sem("xs_ready")
        v_ready = sem("v_ready")
        tq_ready = sem("tq_ready")
        tk_ready = sem("tk_ready")
        guard_ready = sem("guard_ready")
        max_ready = sem("max_ready")
        nb_ready = sem("nb_ready")
        ptp_ready = sem("ptp_ready")
        rec_ready = sem("rec_ready")
        ao_ready = sem("ao_ready")
        aot_ready = sem("aot_ready")
        xm_ready = sem("xm_ready")
        xs2_ready = sem("xs2_ready")
        fdev_ready = sem("fdev_ready")
        fnorm_ready = sem("fnorm_ready")
        fxn_ready = sem("fxn_ready")
        fval_ready = sem("fval_ready")
        fh_ready = sem("fh_ready")
        xnew_ready = sem("xnew_ready")
        total_ready = sem("total_ready")
        dsq_ready = sem("dsq_ready")
        log_ready = sem("log_ready")
        rstd_ready = sem("rstd_ready")
        q0_ready = sem("q0_ready")
        p0_ready = sem("p0_ready")
        aot0_ready = sem("aot0_ready")
        sqq_ready = sem("sqq_ready")
        sqk_ready = sem("sqk_ready")
        log2_ready = sem("log2_ready")
        rn_ready = sem("rn_ready")
        p_ready = sem("p_ready")
        pt_ready = sem("pt_ready")
        fdsq_ready = sem("fdsq_ready")
        flog_ready = sem("flog_ready")
        frstd_ready = sem("frstd_ready")
        fgate_ready = sem("fgate_ready")
        fact_ready = sem("fact_ready")
        qr_ready = sem("qr_ready")
        ka_ready = sem("ka_ready")
        kr_ready = sem("kr_ready")
        consts_in = sem("consts_in")
        hope_in = sem("hope_in")
        x_in = sem("x_in")
        wa_in = sem("wa_in")
        wf_in = sem("wf_in")
        out_in = sem("out_in")
        FIRST = 1

        block = ctx.enter_context(nc.Block())

        def slot(t, n):
            return t[:, bass.ds(n * T, T)]

        def present(p, lag, cur, prev):
            return cur if p >= lag else prev

        def pipeline(eng, step, before_layer=None):
            with eng.Fori(0, L) as l:
                if before_layer:
                    before_layer(l)
                n0 = l * B
                for p in range(NCH):
                    step(n0, n0, 0, p, True, False)
                with eng.Fori(1, B) as s:
                    for p in range(NCH):
                        step(n0, n0 + s, s, p, True, True)
                for p in range(NCH):
                    step(n0, n0 + B, B, p, False, True)

        @block.sync
        def _(sp):
            sp.dma_start(cst[:, :], consts).then_inc(consts_in, 16)
            sp.dma_start(hw[:, :], hope_w).then_inc(hope_in, 16)
            sp.dma_start(hv[:, :], hope_v).then_inc(hope_in, 16)
            sp.dma_start(toep[:, :], toeplitz).then_inc(hope_in, 16)
            for g in range(4):
                nb_ = B // 4
                sp.dma_start(stream[:, g * nb_ * T:(g + 1) * nb_ * T].rearrange("p (b t) -> p b t", t=T),
                             x[g * nb_:(g + 1) * nb_].rearrange("b p t -> p b t")).then_inc(x_in, 16)
            for l in range(L):
                sp.wait_ge(v_done, l * (B * NCH) + FIRST)
                sp.wait_ge(tables_ready, l + FIRST)
                sp.dma_start(wa[:, :], attn_w[l]).then_inc(wa_in, 16)
                sp.wait_ge(xnew_ready, l * B + FIRST)
                sp.dma_start(wf[:, :], ffn_w[l]).then_inc(wf_in, 16)
            for g in range(4):
                sp.wait_ge(total_ready, g + 1 + FIRST)
                sp.dma_start(out[g * 4:(g + 1) * 4].rearrange("b p t -> p b t"),
                             total[:, g, :].rearrange("p (b t) -> p b t", t=T)).then_inc(out_in, 16)
            sp.wait_ge(out_in, 64)

        @block.tensor
        def _(pe):
            mm = nc.tensor.matmul
            for own in (pos_done, mean_done, var_done, q0_done, k0_done, v0_done, s0_done, t0_done, pv0_done,
                        aot0_done, y0_done, q_done, k_done, v_done, s_done, n_done, pv_done, t_done, aot_done,
                        y_done, fmean_done, fvar_done, w1_done, w2_done):
                pe.sem_inc(own, FIRST)

            def norm_sums(src, k, b):
                pe.wait_ge(log_ready, b * 2 + k + FIRST)
                mm(FF[:, 0:T], mean_w[:, :], src, start=True, stop=True).then_inc(mean_done, 1)
                pe.wait_ge(dsq_ready, b * 2 + k + 1 + FIRST)
                mm(FF[:, 0:T], mean_w[:, :], dsq[:, :], start=True, stop=True).then_inc(var_done, 1)

            pe.wait_ge(consts_in, 16)
            pe.wait_ge(hope_in, 48)
            pe.wait_ge(x_in, 64)
            pe.wait_ge(setup_ready, 1 + FIRST)
            for c in range(2):
                last = mm(OO[:, c:c + 1], cst[0:64, C_POS + c * P:C_POS + (c + 1) * P], hv[0:64, V_POS:V_POS + 1],
                          start=True, stop=True)
            last.then_inc(pos_done, 1)
            pe.wait_ge(casts_ready, 3 + FIRST)
            pe.wait_ge(hbias_ready, 1 + FIRST)

            with pe.Fori(0, B) as b:
                norm_sums(slot(stream, b), 0, b)
                pe.wait_ge(ln_ready, b * 2 + 1 + FIRST)
                for r in range(2):
                    pe.wait_ge(q0_ready, b * 2 + r + FIRST)
                    for i in range(2):
                        c = 2 * r + i
                        last = mm(PQ[:, i * T:(i + 1) * T], hw[:, A_Q + c * P:A_Q + (c + 1) * P], xn[:, :],
                                  start=True, stop=True)
                    last.then_inc(q0_done, 1)
                    pe.wait_ge(k0_ready, b * 2 + r + FIRST)
                    for i in range(2):
                        c = 2 * r + i
                        last = mm(PK[:, i * T:(i + 1) * T], hw[:, A_K + c * P:A_K + (c + 1) * P], xn[:, :],
                                  start=True, stop=True)
                    last.then_inc(k0_done, 1)
                    if r == 0:
                        for t in range(TQ):
                            last = mm(NV[:, t * P:(t + 1) * P], xn[:, t * P:(t + 1) * P], hw[:, A_V:A_V + P],
                                      start=True, stop=True)
                        last.then_inc(v0_done, 1)
                pe.wait_ge(q0_ready, b * 2 + 2 + FIRST)
                pe.wait_ge(k0_ready, b * 2 + 2 + FIRST)

                def scores0(h):
                    c, s = h // HPC0, STRIP * (h % HPC0)
                    sc = (S0, S1)[h % 2]
                    if h >= 2:
                        pe.wait_ge(p0_ready, b * H + h - 1 + FIRST)
                    if h < 8:
                        mm(sc[:, 0:S0W], ident, toep[:, h * S0W:(h + 1) * S0W], start=True, stop=False)
                    else:
                        mm(sc[:, 0:S0W], identb[:, :], causalb[:, :], start=True, stop=False)
                    mm(sc[:, 0:P], qh[s:s + STRIP, c, 0:P], kh[s:s + STRIP, c, 0:P], start=False, stop=False)
                    mm(sc[:, P:S0W], qh[s:s + STRIP, c, P:T], kh[s:s + STRIP, c, :],
                       start=False, stop=True).then_inc(s0_done, 1)

                def transposes0(h):
                    tb = (TT, PQ)[h % 2]
                    pe.wait_ge(p0_ready, b * H + h + 1 + FIRST)
                    if h >= 2:
                        pe.wait_ge(pt0_ready, b * H + h - 1 + FIRST)
                    for i in range(3):
                        last = nc.tensor.transpose(tb[:, i * P:(i + 1) * P], prob0[:, h % 2, i * P:(i + 1) * P], ident)
                    last.then_inc(t0_done, 1)

                def values0(h):
                    if h == 0:
                        pe.wait_ge(v0_ready, b + 1 + FIRST)
                        pe.wait_ge(ao0_ready, b + FIRST)
                    pe.wait_ge(pt0_ready, b * H + h + 1 + FIRST)
                    o = OO[:, 0:TQ * H * (HD0 + 1)].rearrange("p (t h e) -> p t h e", t=TQ, h=H)
                    mm(o[:, 0, h, :], pt0[:, h % 2, 0:P], v0[:, 0, h, :], start=True, stop=True)
                    mm(o[:, 1, h, :], pt0[:, h % 2, P:2 * P], v0[:, 0, h, :], start=True, stop=False)
                    mm(o[:, 1, h, :], pt0[:, h % 2, 2 * P:3 * P], v0[:, 1, h, :], start=False, stop=True)\
                        .then_inc(pv0_done, 1)

                for h in range(H + 2):
                    if h < H:
                        scores0(h)
                    if 1 <= h <= H:
                        transposes0(h - 1)
                    if h >= 2:
                        values0(h - 2)
                pe.wait_ge(ao0_ready, b + 1 + FIRST)
                for t in range(TQ):
                    last = nc.tensor.transpose(NV[:, t * P:(t + 1) * P], ao0[:, t, :], ident)
                last.then_inc(aot0_done, 1)
                pe.wait_ge(aot0_ready, b + 1 + FIRST)
                mm(FF[:, 0:T], hw[:, A_P:A_P + P], aot0[:, :], start=True, stop=True).then_inc(y0_done, 1)
                pe.wait_ge(x1_ready, b + 1 + FIRST)
                norm_sums(slot(skip, b), 1, b)

            def step(n0, n, s, p, cur, prev):
                G = n * NCH + p
                if p == 0 and not prev:
                    pe.wait_ge(wa_in, n0 + 16)
                if present(p, 2, cur, prev):
                    pe.wait_ge(p_ready, G - 1 + FIRST)
                    if present(p, 4, cur, prev):
                        pe.wait_ge(aot_ready, G - 3 + FIRST)
                    for t in range(TQ):
                        for i in range(HPC):
                            k = TQ * t + i
                            src = pa[:, p % 2, i, :] if t == 0 else pb[:, p % 2, i, WIN:KB]
                            last = nc.tensor.transpose(TT[:, k * P:(k + 1) * P], src, ident)
                    last.then_inc(t_done, 1)
                if cur:
                    w = p * WCH
                    if p == 0:
                        pe.wait_ge(xs_ready, n + 1 + FIRST)
                    pe.wait_ge(tq_ready, G + FIRST)
                    for i in range(2):
                        last = mm(PQ[:, i * T:(i + 1) * T], wa[:, w + i * P:w + (i + 1) * P], xs[:, :],
                                  start=True, stop=True)
                    last.then_inc(q_done, 1)
                    pe.wait_ge(tk_ready, G + FIRST)
                    for i in range(2):
                        last = mm(PK[:, i * T:(i + 1) * T], wa[:, w + (2 + i) * P:w + (3 + i) * P], xs[:, :],
                                  start=True, stop=True)
                    last.then_inc(k_done, 1)
                    pe.wait_ge(guard_ready, G + FIRST)
                    for t in range(TQ):
                        last = mm(NV[:, t * P:(t + 1) * P], xs[:, t * P:(t + 1) * P],
                                  wa[:, w + 4 * P:w + 5 * P], start=True, stop=True)
                    last.then_inc(v_done, 1)
                if prev:
                    if p == 4:
                        pe.wait_ge(xs2_ready, n + FIRST)
                        mm(FF[:, 0:T], mean_w[:, :], xs2[:, :], start=True, stop=True).then_inc(fmean_done, 1)
                    if p == 5:
                        pe.wait_ge(fdsq_ready, n + FIRST)
                        mm(FF[:, 0:T], mean_w[:, :], dsq[:, :], start=True, stop=True).then_inc(fvar_done, 1)
                    if p == 6:
                        up(n, 1)
                if present(p, 1, cur, prev):
                    pe.wait_ge(p_ready, G - 1 + FIRST)
                    pe.wait_ge(qr_ready, G + FIRST)
                    pe.wait_ge(kr_ready, G + FIRST)
                    par = (p - 1) % 2
                    for sc in (S0, S1):
                        mm(sc[:, 0:2 * KB], identb[:, :], localb[:, :], start=True, stop=False)
                    for i, sc in enumerate((S0, S1)):
                        f = HD * i
                        mm(sc[:, 0:P], qr[f:f + HD, par, 0:P], kr[f:f + HD, par, 0:P], start=False, stop=False)
                    for i, sc in enumerate((S0, S1)):
                        f = HD * i
                        last = mm(sc[:, KB:2 * KB], qr[f:f + HD, par, P:T], kr[f:f + HD, par, P - WIN:T],
                                  start=False, stop=True)
                    last.then_inc(s_done, 1)
                if present(p, 2, cur, prev):
                    par, q4 = p % 2, (p - 2) % 4
                    pe.wait_ge(pt_ready, G - 1 + FIRST)
                    pe.wait_ge(ptp_ready, G - 1 + FIRST)
                    pe.wait_ge(v_ready, G - 1 + FIRST)
                    pe.wait_ge(ao_ready, G - 2 + FIRST)
                    o = OO[:, 0:4 * (HD + 1)].rearrange("p (k e) -> p k e", e=HD + 1)
                    for i in range(HPC):
                        mm(o[:, HPC + i, :], pt[:, par, (2 + i) * P:(3 + i) * P], vs[:, q4, 1, i, :],
                           start=(i == 0), stop=False)
                        mm(o[0:WIN, HPC + i, :], ptp[:, par, i, :], vp[:, q4, i, :], start=False, stop=False)
                    for i in range(HPC):
                        last = mm(o[:, i, :], pt[:, par, i * P:(i + 1) * P], vs[:, q4, 0, i, :],
                                  start=False, stop=(i == HPC - 1))
                    last.then_inc(pv_done, 1)
                if prev and p == 7:
                    pe.wait_ge(fh_ready, n + FIRST)
                    for j in range(FC):
                        last = mm(FF[:, 0:T], wf[:, F_2 + j * P:F_2 + (j + 1) * P], fh[:, j, :],
                                  start=(j == 0), stop=(j == FC - 1))
                    last.then_inc(w2_done, 1)
                if cur:
                    pe.wait_ge(sqk_ready, G + 1 + FIRST)
                    pe.wait_ge(sqq_ready, G + 1 + FIRST)
                    pe.wait_ge(v_ready, G + 1 + FIRST)
                    mm(NV[:, 0:T], blk, sqk[:, :], start=True, stop=True)
                    for t in range(TQ):
                        last = mm(NV[:, T + 2 * t:T + 2 * t + 2], sqq[:, t * P:(t + 1) * P], cst[:, C_BLK:C_BLK + P:HD],
                                  start=True, stop=True)
                    last.then_inc(n_done, 1)
                if prev and p == 3:
                    pe.wait_ge(wf_in, n0 + 16)
                    pe.wait_ge(aot_ready, n * NCH + FIRST)
                    for c in range(NCH):
                        last = mm(FF[:, 0:T], wf[:, F_O + c * P:F_O + (c + 1) * P], aot[:, c, :],
                                  start=(c == 0), stop=(c == NCH - 1))
                    last.then_inc(y_done, 1)
                if present(p, 3, cur, prev):
                    pe.wait_ge(ao_ready, G - 2 + FIRST)
                    if present(p, 2, cur, prev):
                        pe.wait_ge(pt_ready, G - 1 + FIRST)
                    else:
                        pe.wait_ge(aot_ready, G - 3 + FIRST)
                    par = (p - 3) % 2
                    for t in range(TQ):
                        last = nc.tensor.transpose(TT[:, t * P:(t + 1) * P], ao[:, par, t, :], ident)
                    last.then_inc(aot_done, 1)
                if prev and p == 5:
                    up(n, 0)
                if prev and p == 6:
                    up(n, 2)

            def up(n, j):
                pe.wait_ge(fxn_ready, n + FIRST)
                if j:
                    pe.wait_ge(fval_ready, (n - 1) * FC + j + FIRST)
                for i in range(2):
                    w = F_1 + (2 * j + i) * P
                    last = mm(FF[:, i * T:(i + 1) * T], wf[:, w:w + P], xn[:, :], start=True, stop=True)
                last.then_inc(w1_done, 1)

            pipeline(pe, step)

        @block.vector
        def _(dve):
            v = nc.vector
            for own in (setup_ready, casts_ready, hbias_ready, dev_ready, ln_ready, k0_ready, v0_ready,
                        max0_ready, pt0_ready, rec0_ready, ao0_ready, x1_ready, tables_ready, xs_ready, v_ready,
                        tq_ready, tk_ready, guard_ready, max_ready, nb_ready, ptp_ready, rec_ready, ao_ready,
                        aot_ready, xm_ready, xs2_ready, fdev_ready, fnorm_ready, fxn_ready, fval_ready, fh_ready,
                        xnew_ready, total_ready):
                dve.sem_inc(own, FIRST)
            v.memset(mean_w[:, :], 1.0 / D)
            v.memset(eps[:, :], EPS)
            v.memset(v0[:, :, :, :], 1.0)
            v.memset(vs[:, :, :, :, :], 1.0)
            v.memset(vp[:, :, :, :], 1.0)
            v.memset(xs[:, :], 0.0)
            v.memset(xs2[:, :], 0.0).then_inc(setup_ready, 1)
            dve.wait_ge(setup_ready, 1 + FIRST)
            dve.wait_ge(consts_in, 16)
            v.tensor_copy(identb[:, :], ident).then_inc(casts_ready, 1)
            v.tensor_copy(causalb[:, :], cst[:, C_CAUSAL:C_CAUSAL + S0W]).then_inc(casts_ready, 1)
            v.tensor_copy(localb[:, :], cst[:, C_LOCAL:C_LOCAL + 2 * KB]).then_inc(casts_ready, 1)
            dve.wait_ge(hope_in, 48)
            v.tensor_scalar(hbias[:, 0:4], hv[:, V_BQ:V_BQ + 4], HD0 ** -0.5, cst[:, C_ONE:C_ONE + 1],
                            ALU.mult, ALU.add)
            v.tensor_copy(hbias[:, 4:6], hv[:, V_BK:V_BK + 2])
            dve.wait_ge(pos_done, 1 + FIRST)
            v.tensor_tensor(hbias[:, 6:8], OO[:, 0:2], hv[:, V_BK + 2:V_BK + 4], ALU.add).then_inc(hbias_ready, 1)
            dve.wait_ge(hbias_ready, 1 + FIRST)

            def norm(src, dst, k, b):
                dve.wait_ge(mean_done, b * 2 + k + 1 + FIRST)
                dve.wait_ge(ln_ready, b * 2 + k + FIRST)
                v.tensor_tensor(dev[:, :], src, FF[:, 0:T], ALU.subtract).then_inc(dev_ready, 1)
                dve.wait_ge(rstd_ready, b * 2 + k + 1 + FIRST)
                v.tensor_tensor(dst, dev[:, :], rstd[:, :], ALU.mult).then_inc(ln_ready, 1)

            with dve.Fori(0, B) as b:
                norm(slot(stream, b), xn[:, :], 0, b)

                def k_evac(r):
                    dve.wait_ge(k0_done, b * 2 + r + 1 + FIRST)
                    for i in range(2):
                        c = 2 * r + i
                        last = v.tensor_scalar(kh[:, c, :], PK[:, i * T:(i + 1) * T], hbias[:, 4 + c:5 + c], None, ALU.add)
                    last.then_inc(k0_ready, 1)

                k_evac(0)
                dve.wait_ge(v0_done, b + 1 + FIRST)
                v.tensor_copy(v0[:, :, :, 0:HD0], NV[:, 0:T].rearrange("p (t h e) -> p t h e", t=TQ, h=H))\
                    .then_inc(v0_ready, 1)
                k_evac(1)

                def maxima(h):
                    sc = (S0, S1)[h % 2]
                    dve.wait_ge(s0_done, b * H + h + 1 + FIRST)
                    v.tensor_reduce(nmax0[:, h, 0:1], sc[:, 0:P], AX, ALU.max, negate=True)
                    v.tensor_reduce(nmax0[:, h, 1:2], sc[:, P:S0W], AX, ALU.max, negate=True)\
                        .then_inc(max0_ready, 1)

                def pt_evac(h):
                    dve.wait_ge(t0_done, b * H + h + 1 + FIRST)
                    if h >= 2:
                        dve.wait_ge(pv0_done, b * H + h - 1 + FIRST)
                    v.tensor_copy(pt0[:, h % 2, :], (TT, PQ)[h % 2][:, 0:S0W]).then_inc(pt0_ready, 1)

                for h in range(H + 1):
                    if h < H:
                        maxima(h)
                    if h >= 1:
                        pt_evac(h - 1)
                dve.wait_ge(pv0_done, b * H + H + FIRST)
                o = OO[:, 0:TQ * H * (HD0 + 1)].rearrange("p (k e) -> p k e", e=HD0 + 1)
                v.reciprocal(rec0[:, :], o[:, :, HD0]).then_inc(rec0_ready, 1)
                dve.wait_ge(rec0_ready, b + 1 + FIRST)
                v.tensor_tensor(ao0[:, :, :].rearrange("p t (h e) -> p (t h) e", e=HD0), o[:, :, 0:HD0],
                                rec0[:, :].unsqueeze(2).to_broadcast([P, TQ * H, HD0]), ALU.mult)\
                    .then_inc(ao0_ready, 1)
                dve.wait_ge(y0_done, b + 1 + FIRST)
                v.scalar_tensor_tensor(slot(skip, b), FF[:, 0:T], hv[:, V_BP:V_BP + 1], slot(stream, b),
                                       ALU.add, ALU.add).then_inc(x1_ready, 1)
                norm(slot(skip, b), slot(stream, b), 1, b)

            def before_layer(l):
                dve.wait_ge(wa_in, l * 16 + 16)
                sc = NCH * WCH
                for i in range(2):
                    v.tensor_scalar(csq[:, i * T:(i + 1) * T], cst[:, C_RQ + i * T:C_RQ + (i + 1) * T],
                                    wa[:, sc + i:sc + i + 1], None, ALU.mult)
                for i in range(2):
                    last = v.tensor_scalar(csk[:, i * T:(i + 1) * T], cst[:, C_RK + i * T:C_RK + (i + 1) * T],
                                           wa[:, sc + 2 + i:sc + 3 + i], None, ALU.mult)
                last.then_inc(tables_ready, 1)
                dve.wait_ge(tables_ready, l + 1 + FIRST)

            def step(n0, n, s, p, cur, prev):
                G = n * NCH + p
                if cur and p == 0:
                    dve.wait_ge(v_done, G + FIRST)
                    dve.wait_ge(xnew_ready, n0 + FIRST)
                    src = slot(stream, s)
                    v.tensor_copy(xs[0:HD, :], src[0:HD, :])
                    v.tensor_copy(xs[HD:P, 1:T], src[HD:P, 0:T - 1]).then_inc(xs_ready, 1)
                if present(p, 2, cur, prev):
                    dve.wait_ge(p_ready, G - 1 + FIRST)
                    if present(p, 4, cur, prev):
                        dve.wait_ge(pv_done, G - 3 + FIRST)
                    v.transpose(ptp[:, p % 2, :, :], pb[0:WIN, p % 2, :, 0:WIN]).then_inc(ptp_ready, 1)
                if prev and p == 6:
                    value(n, 0)
                if prev and p == 7:
                    value(n, 2)
                if cur:
                    dve.wait_ge(sqq_ready, G + 1 + FIRST)
                    if p >= 2 or prev:
                        dve.wait_ge(qr_ready, G - 1 + FIRST)
                    v.tensor_tensor(tq[:, p % 2, :], PQ[:, :], csq[:, :], ALU.mult).then_inc(tq_ready, 1)
                    dve.wait_ge(sqk_ready, G + 1 + FIRST)
                    if p >= 2 or prev:
                        dve.wait_ge(ka_ready, G - 1 + FIRST)
                    v.tensor_tensor(tk[:, p % 2, :], PK[:, :], csk[:, :], ALU.mult).then_inc(tk_ready, 1)
                    dve.wait_ge(v_done, G + 1 + FIRST)
                    nv = NV[:, 0:T].rearrange("p (t i e) -> p t i e", t=TQ, i=HPC)
                    v.tensor_copy(vs[:, p % 4, :, :, 0:HD], nv)
                    v.tensor_copy(vp[:, p % 4, :, 0:HD], nv[P - WIN:P, 0, :, :]).then_inc(v_ready, 1)
                if prev and p == 7:
                    dve.wait_ge(fact_ready, n + FIRST)
                    dve.wait_ge(fval_ready, n * FC + FIRST)
                    v.tensor_tensor(fh[:, :, :], fval[:, :, :], fact[:, :, :], ALU.mult).then_inc(fh_ready, 1)
                if present(p, 1, cur, prev):
                    par = (p - 1) % 2
                    dve.wait_ge(s_done, G + FIRST)
                    dve.wait_ge(nb_ready, G - 1 + FIRST)
                    v.tensor_reduce(nm[:, 0:2], S0[:, 0:2 * KB].rearrange("p (i j) -> p i j", j=KB), AX, ALU.max,
                                    negate=True)
                    v.tensor_reduce(nm[:, 2:4], S1[:, 0:2 * KB].rearrange("p (i j) -> p i j", j=KB), AX, ALU.max,
                                    negate=True).then_inc(max_ready, 1)
                    dve.wait_ge(max_ready, G + FIRST)
                    dve.wait_ge(rn_ready, G + FIRST)
                    v.tensor_tensor(nb[:, par, :].rearrange("p (i t) -> p i t", t=TQ),
                                    nm[:, :].rearrange("p (i t) -> p i t", t=TQ),
                                    rn[:, par, T:T + 4].rearrange("p (t i) -> p i t", i=HPC), ALU.mult).then_inc(nb_ready, 1)
                if prev and p == 4:
                    dve.wait_ge(fmean_done, n + FIRST)
                    v.tensor_tensor(dev[:, :], xs2[:, :], FF[:, 0:T], ALU.subtract).then_inc(fdev_ready, 1)
                if present(p, 2, cur, prev):
                    par = p % 2
                    dve.wait_ge(pv_done, G - 1 + FIRST)
                    if present(p, 4, cur, prev):
                        dve.wait_ge(aot_done, G - 3 + FIRST)
                    o = OO[:, 0:4 * (HD + 1)].rearrange("p (k e) -> p k e", e=HD + 1)
                    dve.wait_ge(ao_ready, G - 2 + FIRST)
                    v.reciprocal(rec[:, :], o[:, :, HD]).then_inc(rec_ready, 1)
                    dve.wait_ge(rec_ready, G - 1 + FIRST)
                    v.tensor_tensor(ao[:, par, :, :].rearrange("p t (i e) -> p (t i) e", e=HD), o[:, :, 0:HD],
                                    rec[:, :].unsqueeze(2).to_broadcast([P, 4, HD]), ALU.mult)\
                        .then_inc(ao_ready, 1)
                if prev and p == 5:
                    dve.wait_ge(frstd_ready, n + FIRST)
                    v.scalar_tensor_tensor(dev[:, :], dev[:, :], wf[:, F_G:F_G + 1], rstd[:, :], ALU.mult, ALU.mult)\
                        .then_inc(fnorm_ready, 1)
                    dve.wait_ge(fnorm_ready, n + FIRST)
                    v.tensor_scalar(xn[:, :], dev[:, :], wf[:, F_B:F_B + 1], None, ALU.add)\
                        .then_inc(fxn_ready, 1)
                if prev and p == 6:
                    value(n, 1)
                if cur:
                    dve.wait_ge(n_done, G + 1 + FIRST)
                    if p >= 1 or prev:
                        dve.wait_ge(log2_ready, G + FIRST)
                    v.tensor_scalar(ng[:, :], NV[:, 0:T + 4], NORM_GUARD, None, ALU.max).then_inc(guard_ready, 1)
                if present(p, 3, cur, prev):
                    c = (p - 3) % NCH
                    dve.wait_ge(aot_done, G - 2 + FIRST)
                    if c == 0 and prev:
                        dve.wait_ge(y_done, n + FIRST)
                    v.tensor_copy(aot[:, c, :], TT[:, 0:T]).then_inc(aot_ready, 1)
                if prev and p == 3:
                    dve.wait_ge(y_done, n + FIRST)
                    dve.wait_ge(xnew_ready, n - 1 + FIRST)
                    v.tensor_tensor(xm[:, :], FF[:, 0:T], slot(stream, s - 1), ALU.add).then_inc(xm_ready, 1)
                    dve.wait_ge(xm_ready, n + FIRST)
                    v.tensor_copy(xs2[0:HD, :], xm[0:HD, :])
                    v.tensor_copy(xs2[HD:P, 1:T], xm[HD:P, 0:T - 1]).then_inc(xs2_ready, 1)
                if prev and p == 7:
                    dve.wait_ge(w2_done, n + FIRST)
                    v.scalar_tensor_tensor(slot(stream, s - 1), FF[:, 0:T], wf[:, F_B2:F_B2 + 1], xm[:, :],
                                           ALU.add, ALU.add).then_inc(xnew_ready, 1)

            def value(n, j):
                dve.wait_ge(fgate_ready, (n - 1) * FC + j + 1 + FIRST)
                v.tensor_scalar(fval[:, j, :], FF[:, 0:T], wf[:, F_B1 + 2 * j:F_B1 + 2 * j + 1], None, ALU.add)\
                    .then_inc(fval_ready, 1)

            dve.wait_ge(ln_ready, 2 * B + FIRST)
            pipeline(dve, step, before_layer)
            dve.wait_ge(xnew_ready, L * B + FIRST)
            for g in range(4):
                w = B * T // 4
                v.tensor_tensor(total[:, g, :], stream[:, g * w:(g + 1) * w], skip[:, g * w:(g + 1) * w], ALU.add)\
                    .then_inc(total_ready, 1)

        @block.scalar
        def _(act):
            a = nc.scalar.activation
            for own in (dsq_ready, log_ready, rstd_ready, q0_ready, p0_ready, aot0_ready, sqq_ready, sqk_ready,
                        log2_ready, rn_ready, p_ready, pt_ready, fdsq_ready, flog_ready, frstd_ready,
                        fgate_ready, fact_ready):
                act.sem_inc(own, FIRST)
            nc.scalar.preload_act_table_set("natural_log_exp_and_others")
            act.wait_ge(setup_ready, 1 + FIRST)
            act.wait_ge(hbias_ready, 1 + FIRST)

            def norm(k, b):
                act.wait_ge(dev_ready, b * 2 + k + 1 + FIRST)
                a(dsq[:, :], dev[:, :], ACT.Square).then_inc(dsq_ready, 1)
                act.wait_ge(var_done, b * 2 + k + 1 + FIRST)
                a(logv[:, :], FF[:, 0:T], ACT.Ln, bias=eps[:, 0:1]).then_inc(log_ready, 1)
                act.wait_ge(log_ready, b * 2 + k + 1 + FIRST)
                a(rstd[:, :], logv[:, :], ACT.Exp, scale=-0.5).then_inc(rstd_ready, 1)

            with act.Fori(0, B) as b:
                norm(0, b)
                for r in range(2):
                    act.wait_ge(q0_done, b * 2 + r + 1 + FIRST)
                    for i in range(2):
                        c = 2 * r + i
                        last = a(qh[:, c, :], PQ[:, i * T:(i + 1) * T], ACT.Identity, bias=hbias[:, c:c + 1],
                                 scale=HD0 ** -0.5)
                    last.then_inc(q0_ready, 1)
                for h in range(H):
                    sc = (S0, S1)[h % 2]
                    act.wait_ge(max0_ready, b * H + h + 1 + FIRST)
                    if h >= 2:
                        act.wait_ge(t0_done, b * H + h - 1 + FIRST)
                    a(prob0[:, h % 2, 0:P], sc[:, 0:P], ACT.Exp, bias=nmax0[:, h, 0:1])
                    a(prob0[:, h % 2, P:S0W], sc[:, P:S0W], ACT.Exp, bias=nmax0[:, h, 1:2]).then_inc(p0_ready, 1)
                act.wait_ge(aot0_done, b + 1 + FIRST)
                a(aot0[:, :], NV[:, 0:T], ACT.Identity, bias=hv[:, V_BV:V_BV + 1]).then_inc(aot0_ready, 1)
                norm(1, b)

            def step(n0, n, s, p, cur, prev):
                G = n * NCH + p
                if present(p, 1, cur, prev):
                    par = (p - 1) % 2
                    act.wait_ge(guard_ready, G + FIRST)
                    act.wait_ge(rn_ready, G - 1 + FIRST)
                    a(lg[:, :], ng[:, :], ACT.Ln).then_inc(log2_ready, 1)
                    act.wait_ge(log2_ready, G + FIRST)
                    if present(p, 3, cur, prev):
                        act.wait_ge(kr_ready, G - 2 + FIRST)
                    a(rn[:, par, :], lg[:, :], ACT.Exp, scale=-0.5).then_inc(rn_ready, 1)
                if prev and p == 6:
                    gate(n, 0)
                if present(p, 2, cur, prev):
                    act.wait_ge(t_done, G - 1 + FIRST)
                    if present(p, 4, cur, prev):
                        act.wait_ge(pv_done, G - 3 + FIRST)
                    a(pt[:, p % 2, :], TT[:, :], ACT.Copy).then_inc(pt_ready, 1)
                if cur:
                    act.wait_ge(q_done, G + 1 + FIRST)
                    act.wait_ge(n_done, G + FIRST)
                    a(sqq[:, :], PQ[:, 0:T], ACT.Square).then_inc(sqq_ready, 1)
                    act.wait_ge(k_done, G + 1 + FIRST)
                    a(sqk[:, :], PK[:, 0:T], ACT.Square).then_inc(sqk_ready, 1)
                if prev and p == 7:
                    gate(n, 2)
                    act.wait_ge(fgate_ready, n * FC + FIRST)
                    a(fact[:, :, :], fgate[:, :, :], ACT.Gelu).then_inc(fact_ready, 1)
                    nc.scalar.preload_act_table_set("natural_log_exp_and_others")
                if present(p, 1, cur, prev):
                    par = (p - 1) % 2
                    act.wait_ge(nb_ready, G + FIRST)
                    if present(p, 3, cur, prev):
                        act.wait_ge(t_done, G - 2 + FIRST)
                        act.wait_ge(ptp_ready, G - 2 + FIRST)
                    for i, sc in enumerate((S0, S1)):
                        k, r = TQ * i, T + i
                        a(pa[:, par, i, :], sc[:, 0:P], ACT.Exp, bias=nb[:, par, k:k + 1],
                          scale=rn[:, par, r:r + 1])
                        k, r = k + 1, r + HPC
                        last = a(pb[:, par, i, :], sc[:, KB:2 * KB], ACT.Exp, bias=nb[:, par, k:k + 1],
                                 scale=rn[:, par, r:r + 1])
                    last.then_inc(p_ready, 1)
                if prev and p == 4:
                    act.wait_ge(fdev_ready, n + FIRST)
                    a(dsq[:, :], dev[:, :], ACT.Square).then_inc(fdsq_ready, 1)
                if prev and p == 5:
                    act.wait_ge(fvar_done, n + FIRST)
                    a(logv[:, :], FF[:, 0:T], ACT.Ln, bias=eps[:, 0:1]).then_inc(flog_ready, 1)
                    act.wait_ge(flog_ready, n + FIRST)
                    a(rstd[:, :], logv[:, :], ACT.Exp, scale=-0.5).then_inc(frstd_ready, 1)
                if prev and p == 6:
                    gate(n, 1)

            def gate(n, j):
                act.wait_ge(w1_done, (n - 1) * FC + j + 1 + FIRST)
                b1 = F_B1 + 2 * j + 1
                a(fgate[:, j, :], FF[:, T:2 * T], ACT.Identity, bias=wf[:, b1:b1 + 1]).then_inc(fgate_ready, 1)

            pipeline(act, step)

        @block.gpsimd
        def _(pool):
            g = nc.gpsimd
            for own in (qr_ready, ka_ready, kr_ready):
                pool.sem_inc(own, FIRST)

            def step(n0, n, s, p, cur, prev):
                G = n * NCH + p
                if not cur:
                    return
                par = p % 2
                pool.wait_ge(tq_ready, G + 1 + FIRST)
                if p >= 2 or prev:
                    pool.wait_ge(s_done, G - 1 + FIRST)
                g.tensor_tensor(qr[:, par, :], tq[:, par, 0:T], tq[:, par, T:2 * T], ALU.add).then_inc(qr_ready, 1)
                pool.wait_ge(tk_ready, G + 1 + FIRST)
                g.tensor_tensor(ka[:, par, :], tk[:, par, 0:T], tk[:, par, T:2 * T], ALU.add).then_inc(ka_ready, 1)
                pool.wait_ge(ka_ready, G + 1 + FIRST)
                pool.wait_ge(rn_ready, G + 1 + FIRST)
                g.tensor_tensor(kr[:, par, :], ka[:, par, :], rn[:, par, 0:T], ALU.mult).then_inc(kr_ready, 1)

            pipeline(pool, step)


def constants():
    c = np.zeros((P, C_N), np.float32)
    c[:, C_ID:C_ID + P] = np.eye(P, dtype=np.float32)
    i = np.arange(P)[:, None]
    ch = np.where(i >= np.arange(P)[None], 0.0, MASKED)
    cw = np.where(i + P >= np.arange(T)[None], 0.0, MASKED)
    c[:, C_CAUSAL:C_CAUSAL + S0W] = np.concatenate([ch, cw], 1)
    d0 = i - np.arange(P)[None]
    d1 = i + WIN - np.arange(KB)[None]
    m0, m1 = (np.where((d >= 0) & (d <= WIN), 0.0, MASKED) for d in (d0, d1))
    none = np.full((P, KB - P), MASKED)
    c[:, C_LOCAL:C_LOCAL + 2 * KB] = np.concatenate([m0, none, m1], 1)
    half = np.arange(0, HD, 2, dtype=np.float32)
    inv_freq = (np.float32(1.0) / np.float32(10000.0) ** (half / np.float32(HD))).astype(np.float32)
    t = np.arange(T, dtype=np.float32)
    fr = t[:, None] * inv_freq[None]
    fr = np.concatenate([fr, fr], 1)
    base = ((half + np.float32(0.4 * HD)) / np.float32(1.4 * HD)).astype(np.float32)
    scale = base[None].astype(np.float64) ** ((t - T // 2) / np.float32(WIN // 2))[:, None].astype(np.float64)
    scale = np.concatenate([scale, scale], 1)
    cos, sin = np.cos(fr.astype(np.float64)), np.sin(fr.astype(np.float64))
    sign = np.where(np.arange(HD) < HD // 2, -1.0, 1.0)[None]
    for at, sc in ((C_RQ, 8.0 * scale), (C_RK, 1.0 / scale)):
        c[:, at:at + T] = np.tile((cos * sc).T, (2, 1))
        c[:, at + T:at + 2 * T] = np.tile((sin * sign * sc).T, (2, 1))
    c[:, C_BLK:C_BLK + P] = np.kron(np.eye(2), np.ones((HD, HD)))
    rows = np.arange(HPC0) * STRIP + HD0
    c[rows, C_ONE] = 1.0
    for ck in range(2):
        for s in range(HPC0):
            hh = HPC0 * ck + s
            c[8 * hh:8 * hh + 8, C_POS + ck * P + s * STRIP + HD0] = 1.0
    dim = D // 2
    fq = (1.0 / 1250 ** (np.arange(dim, dtype=np.float64) / dim))[:dim - D // 4].astype(np.float32)
    dd = np.arange(-(T - 1), T, dtype=np.float32)
    th = dd[:, None] * fq[None]
    pv = np.cos(th).astype(np.float32) + np.sin(th).astype(np.float32)
    ph = pv.reshape(2 * T - 1, 8, 4).sum(-1)
    tp = np.zeros((P, 8, S0W), np.float32)
    for h in range(8):
        a0 = np.where(ch == 0, ph[i - np.arange(P)[None] + T - 1, h], MASKED)
        a1 = np.where(cw == 0, ph[i + P - np.arange(T)[None] + T - 1, h], MASKED)
        tp[:, h] = np.concatenate([a0, a1], 1)
    return c, tp.reshape(P, 8 * S0W)


def kernel(**inputs):
    import concourse.bacc as bacc
    from concourse.bass_utils import run_bass_kernel_spmd

    g = {k: np.asarray(v) for k, v in inputs.items()}
    f = np.float32
    consts, toeplitz = constants()
    x = np.ascontiguousarray(g["L0_attn_x"].transpose(0, 2, 1))
    wqkv = g["L0_attn_w_qkv"].reshape(3, NC0, HPC0, HD0, D)
    bqkv = g["L0_attn_b_qkv"].reshape(3, NC0, HPC0, HD0)
    hope_w = np.zeros((P, A_N), f)
    hope_v = np.zeros((P, V_N), f)
    for at, bt, k in ((A_Q, V_BQ, 0), (A_K, V_BK, 1)):
        w = np.zeros((NC0, HPC0, STRIP, D), f)
        w[:, :, :HD0] = wqkv[k]
        hope_w[:, at:at + NC0 * P] = w.reshape(NC0 * P, D).T
        bb = np.zeros((NC0, HPC0, STRIP), f)
        bb[:, :, :HD0] = bqkv[k]
        hope_v[:, bt:bt + NC0] = bb.reshape(NC0, P).T
    hope_w[:, A_V:A_V + D] = g["L0_attn_w_qkv"][2 * D:].T
    hope_w[:, A_P:A_P + D] = g["L0_attn_w_proj"].T
    hope_v[:, V_BV] = g["L0_attn_b_qkv"][2 * D:]
    hope_v[:, V_BP] = g["L0_attn_b_proj"]
    hope_v[:64, V_POS] = g["L0_attn_pos_independent"].reshape(64)
    partner = (np.arange(HD) + HD // 2) % HD
    w = g["L0_ffn_Wqkv"].reshape(L, D, 3, NCH, HPC, HD)
    q, k, v = w[:, :, 0], w[:, :, 1], w[:, :, 2]
    attn_w = np.zeros((L, P, WA_N), f)
    parts = np.stack([q, q[..., partner], k, k[..., partner], v], 3)
    attn_w[:, :, :NCH * WCH] = parts.reshape(L, D, NCH * WCH)
    for i, (nm, pt) in enumerate((("q", 0), ("q", 1), ("k", 0), ("k", 1))):
        sc = g[f"L0_ffn_{nm}_scale"]
        sc = sc[:, partner] if pt else sc
        attn_w[:, :HD, NCH * WCH + i] = sc
        attn_w[:, HD:, NCH * WCH + i] = sc
    ffn_w = np.zeros((L, P, WF_N), f)
    ffn_w[:, :, F_O:F_O + NCH * P] = g["L0_ffn_Wo"].reshape(L, NCH, P, D).transpose(0, 2, 1, 3).reshape(L, P, NCH * D)
    w1 = np.zeros((L, D, FC, 2, P), f)
    b1 = np.zeros((L, FC, 2, P), f)
    w2 = np.zeros((L, FC * P, D), f)
    w2[:, :FI] = g["L0_ffn_W2"]
    for j in range(FC):
        e = min(P, FI - j * P)
        for i in range(2):
            at = i * FI + j * P
            w1[:, :, j, i, :e] = g["L0_ffn_W1"][:, :, at:at + e]
            b1[:, j, i, :e] = g["L0_ffn_b1"][:, at:at + e]
    ffn_w[:, :, F_1:F_1 + 2 * FC * P] = w1.reshape(L, D, 2 * FC * P)
    ffn_w[:, :, F_2:F_2 + FC * P] = w2.reshape(L, FC, P, D).transpose(0, 2, 1, 3).reshape(L, P, FC * D)
    ffn_w[:, :, F_G] = g["L0_ffn_ln_g"]
    ffn_w[:, :, F_B] = g["L0_ffn_ln_b"]
    ffn_w[:, :, F_B1:F_B1 + 2 * FC] = b1.reshape(L, 2 * FC, P).transpose(0, 2, 1)
    ffn_w[:, :, F_B2] = g["L0_ffn_b2"]

    nc = bacc.Bacc("TRN2", target_bir_lowering=False, num_devices=1)
    arrays, args = {}, []
    for name, arr in (("x", x), ("consts", consts), ("toeplitz", toeplitz), ("hope_w", hope_w), ("hope_v", hope_v),
                      ("attn_w", attn_w), ("ffn_w", ffn_w)):
        arr = np.ascontiguousarray(arr)
        arrays[f"in_{name}"] = arr
        args.append(nc.dram_tensor(f"in_{name}", arr.shape, mybir.dt.from_np(arr.dtype), kind="ExternalInput").ap())
    args.append(nc.dram_tensor("out_y", (B, D, T), F32, kind="ExternalOutput").ap())
    sequence_kernel(nc, *args)
    r = run_bass_kernel_spmd(nc, [arrays], core_ids=[0])
    return np.ascontiguousarray(r.results[0]["out_y"].transpose(0, 2, 1))
```

```python
from contextlib import ExitStack

import concourse.bass as bass
import numpy as np
from concourse import mybir

F32 = mybir.dt.float32
BF16 = mybir.dt.bfloat16
ALU = mybir.AluOpType
ACT = mybir.ActivationFunctionType
AX = mybir.AxisListType.X

P = 128
B, T, D = 16, 256, 128
TQ = T // P
H = 16
HD0 = D // H
STRIP = 32
HPC0 = P // STRIP
NC0 = H // HPC0
HD = 64
HPC = P // HD
NCH = H // HPC
L = 6
WIN = 32
FI = 341
FC = 3
WO_AT = {1: (0, 4), 2: (4, 5), 3: (5, 6), 4: (6, 8)}
KB = P + WIN
S0W = 3 * P
EPS = 1e-5
MASKED = -1e30
NORM_GUARD = 1e-24

SWAP = [(r + 16) % 32 for r in range(32)]
ORDER = [16 * a + r if r < 16 else HD // 2 + 16 * a + r - 16 for a in range(2) for r in range(32)]

C_ID, C_CAUSAL, C_LOCAL, C_COS, C_SIN, C_BLK, C_ONE, C_POS = 0, 128, 512, 832, 1344, 1856, 1984, 1985
C_N = C_POS + 2 * P
A_Q, A_K, A_V, A_P, A_N = 0, 512, 1024, 1152, 1280
V_BQ, V_BK, V_BV, V_BP, V_POS, V_N = 0, 4, 8, 9, 10, 11
WCH = 3 * P
WA_N = NCH * WCH + 4
F_O, F_1, F_2, F_V = 0, 1024, 1792, 2176
F_G, F_B, F_B1, F_B2 = F_V, F_V + 1, F_V + 2, F_V + 8
WF_N = F_V + 9


def sequence_kernel(nc, x, consts, toeplitz, hope_w, hope_v, attn_w, ffn_w, out):
    with ExitStack() as ctx:
        def sb(name, shape, dt=F32):
            return ctx.enter_context(nc.sbuf_tensor(name, shape, dt))

        def sem(name):
            return ctx.enter_context(nc.semaphore(name))

        stream = sb("stream", [P, B * T])
        skip = sb("skip", [P, B * T])
        cst = sb("cst", [P, C_N])
        toep = sb("toep", [P, 8 * S0W])
        hw = sb("hw", [P, A_N])
        hv = sb("hv", [P, V_N])
        wa = sb("wa", [P, WA_N])
        wf = sb("wf", [P, WF_N])
        identb = sb("identb", [P, P], BF16)
        causalb = sb("causalb", [P, S0W], BF16)
        localb = sb("localb", [P, 2 * KB], BF16)
        mean_w = sb("mean_w", [P, P])
        eps = sb("eps", [P, 1])
        hbias = sb("hbias", [P, 8])
        qh = sb("qh", [P, NC0, T])
        kh = sb("kh", [P, NC0, T])
        v0 = sb("v0", [P, TQ, H, HD0 + 1])
        nmax0 = sb("nmax0", [P, H, TQ])
        prob0 = sb("prob0", [P, 2, S0W])
        pt0 = sb("pt0", [P, 2, S0W])
        rec0 = sb("rec0", [P, TQ * H])
        ao0 = sb("ao0", [P, TQ, D])
        aot0 = sb("aot0", [P, T])
        dev = sb("dev", [P, T])
        dsq = sb("dsq", [P, T])
        logv = sb("logv", [P, T])
        rstd = sb("rstd", [P, T])
        xn = sb("xn", [P, T])
        xs = sb("xs", [P, T])
        cosw = sb("cosw", [P, 2 * T])
        sinw = sb("sinw", [P, 2 * T])
        sq = sb("sq", [P, 2 * T])
        qkc = sb("qkc", [P, 2, 2 * T])
        qkx = sb("qkx", [P, 2, 2 * T])
        qks = sb("qks", [P, 2, 2 * T])
        qkr = sb("qkr", [P, 2, 2 * T])
        kr = sb("kr", [P, 2, T])
        ng = sb("ng", [P, T + 4])
        lg = sb("lg", [P, T + 4])
        rn = sb("rn", [P, 2, T + 4])
        nm = sb("nm", [P, 4])
        nb = sb("nb", [P, 2, 4])
        pa = sb("pa", [P, 2, HPC, P])
        pb = sb("pb", [P, 2, HPC, KB])
        pt = sb("pt", [P, 2, 4 * P])
        ptp = sb("ptp", [WIN, 2, HPC, WIN])
        vs = sb("vs", [P, 4, TQ, HPC, HD + 1])
        vp = sb("vp", [WIN, 4, HPC, HD + 1])
        rec = sb("rec", [P, 4])
        ao = sb("ao", [P, 2, TQ, P])
        aot = sb("aot", [P, NCH, T])
        xm = sb("xm", [P, T])
        xs2 = sb("xs2", [P, T])
        fval = sb("fval", [P, FC, T])
        fgate = sb("fgate", [P, FC, T])
        fact = sb("fact", [P, FC, T])
        fh = sb("fh", [P, FC, T])
        total = sb("total", [P, 4, T * B // 4])

        def bank(name):
            return ctx.enter_context(nc.psum_tensor(name, [P, 512], F32))

        QK0, QK1, NV, S0, S1, TT, OO, FF = [bank(n) for n in ("QK0", "QK1", "NV", "S0", "S1", "TT", "OO", "FF")]

        ident = cst[:, C_ID:C_ID + P]
        blk = cst[:, C_BLK:C_BLK + P]

        pos_done = sem("pos_done")
        mean_done = sem("mean_done")
        var_done = sem("var_done")
        q0_done = sem("q0_done")
        k0_done = sem("k0_done")
        v0_done = sem("v0_done")
        s0_done = sem("s0_done")
        t0_done = sem("t0_done")
        pv0_done = sem("pv0_done")
        aot0_done = sem("aot0_done")
        y0_done = sem("y0_done")
        qk_done = sem("qk_done")
        v_done = sem("v_done")
        s_done = sem("s_done")
        n_done = sem("n_done")
        pv_done = sem("pv_done")
        t_done = sem("t_done")
        aot_done = sem("aot_done")
        y_done = sem("y_done")
        fmean_done = sem("fmean_done")
        fvar_done = sem("fvar_done")
        w1_done = sem("w1_done")
        w2_done = sem("w2_done")
        setup_ready = sem("setup_ready")
        casts_ready = sem("casts_ready")
        hbias_ready = sem("hbias_ready")
        dev_ready = sem("dev_ready")
        ln_ready = sem("ln_ready")
        k0_ready = sem("k0_ready")
        v0_ready = sem("v0_ready")
        max0_ready = sem("max0_ready")
        pt0_ready = sem("pt0_ready")
        rec0_ready = sem("rec0_ready")
        ao0_ready = sem("ao0_ready")
        x1_ready = sem("x1_ready")
        tables_ready = sem("tables_ready")
        xs_ready = sem("xs_ready")
        v_ready = sem("v_ready")
        qkc_ready = sem("qkc_ready")
        qkx_ready = sem("qkx_ready")
        guard_ready = sem("guard_ready")
        max_ready = sem("max_ready")
        nb_ready = sem("nb_ready")
        ptp_ready = sem("ptp_ready")
        rec_ready = sem("rec_ready")
        ao_ready = sem("ao_ready")
        xm_ready = sem("xm_ready")
        xs2_ready = sem("xs2_ready")
        fdev_ready = sem("fdev_ready")
        fnorm_ready = sem("fnorm_ready")
        fxn_ready = sem("fxn_ready")
        fval_ready = sem("fval_ready")
        fh_ready = sem("fh_ready")
        xnew_ready = sem("xnew_ready")
        total_ready = sem("total_ready")
        dsq_ready = sem("dsq_ready")
        log_ready = sem("log_ready")
        rstd_ready = sem("rstd_ready")
        q0_ready = sem("q0_ready")
        p0_ready = sem("p0_ready")
        aot0_ready = sem("aot0_ready")
        sq_ready = sem("sq_ready")
        log2_ready = sem("log2_ready")
        rn_ready = sem("rn_ready")
        p_ready = sem("p_ready")
        pt_ready = sem("pt_ready")
        aot_ready = sem("aot_ready")
        fdsq_ready = sem("fdsq_ready")
        flog_ready = sem("flog_ready")
        frstd_ready = sem("frstd_ready")
        fgate_ready = sem("fgate_ready")
        fact_ready = sem("fact_ready")
        qks_ready = sem("qks_ready")
        qkr_ready = sem("qkr_ready")
        kr_ready = sem("kr_ready")
        consts_in = sem("consts_in")
        hope_in = sem("hope_in")
        x_in = sem("x_in")
        wa_in = sem("wa_in")
        wf_in = sem("wf_in")
        out_in = sem("out_in")
        FIRST = 1

        block = ctx.enter_context(nc.Block())

        def slot(t, n):
            return t[:, bass.ds(n * T, T)]

        def present(p, lag, k0, k1):
            return k0 if p >= lag else k1

        def pipeline(eng, step, before_layer=None):
            with eng.Fori(0, L) as l:
                if before_layer:
                    before_layer(l)
                n0 = l * B
                for p in range(NCH):
                    step(n0, n0, 0, p, True, False, False)
                for p in range(NCH):
                    step(n0, n0 + 1, 1, p, True, True, False)
                with eng.Fori(2, B) as s:
                    for p in range(NCH):
                        step(n0, n0 + s, s, p, True, True, True)
                for p in range(NCH):
                    step(n0, n0 + B, B, p, False, True, True)
                step(n0, n0 + B + 1, B + 1, 0, False, False, True)

        @block.sync
        def _(sp):
            sp.dma_start(cst[:, :], consts).then_inc(consts_in, 16)
            sp.dma_start(hw[:, :], hope_w).then_inc(hope_in, 16)
            sp.dma_start(hv[:, :], hope_v).then_inc(hope_in, 16)
            sp.dma_start(toep[:, :], toeplitz).then_inc(hope_in, 16)
            for g in range(4):
                nb_ = B // 4
                sp.dma_start(stream[:, g * nb_ * T:(g + 1) * nb_ * T].rearrange("p (b t) -> p b t", t=T),
                             x[g * nb_:(g + 1) * nb_].rearrange("b p t -> p b t")).then_inc(x_in, 16)
            for l in range(L):
                sp.wait_ge(v_done, l * (B * NCH) + FIRST)
                sp.wait_ge(tables_ready, l + FIRST)
                sp.dma_start(wa[:, :], attn_w[l]).then_inc(wa_in, 16)
                sp.wait_ge(xnew_ready, l * B + FIRST)
                sp.dma_start(wf[:, :], ffn_w[l]).then_inc(wf_in, 16)
            for g in range(4):
                sp.wait_ge(total_ready, g + 1 + FIRST)
                sp.dma_start(out[g * 4:(g + 1) * 4].rearrange("b p t -> p b t"),
                             total[:, g, :].rearrange("p (b t) -> p b t", t=T)).then_inc(out_in, 16)
            sp.wait_ge(out_in, 64)

        @block.tensor
        def _(pe):
            mm = nc.tensor.matmul
            for own in (pos_done, mean_done, var_done, q0_done, k0_done, v0_done, s0_done, t0_done, pv0_done,
                        aot0_done, y0_done, qk_done, v_done, s_done, n_done, pv_done, t_done, aot_done, y_done,
                        fmean_done, fvar_done, w1_done, w2_done):
                pe.sem_inc(own, FIRST)

            def norm_sums(src, k, b):
                pe.wait_ge(log_ready, b * 2 + k + FIRST)
                mm(FF[:, 0:T], mean_w[:, :], src, start=True, stop=True).then_inc(mean_done, 1)
                pe.wait_ge(dsq_ready, b * 2 + k + 1 + FIRST)
                mm(FF[:, 0:T], mean_w[:, :], dsq[:, :], start=True, stop=True).then_inc(var_done, 1)

            pe.wait_ge(consts_in, 16)
            pe.wait_ge(hope_in, 48)
            pe.wait_ge(x_in, 64)
            pe.wait_ge(setup_ready, 1 + FIRST)
            for c in range(2):
                last = mm(OO[:, c:c + 1], cst[0:64, C_POS + c * P:C_POS + (c + 1) * P], hv[0:64, V_POS:V_POS + 1],
                          start=True, stop=True)
            last.then_inc(pos_done, 1)
            pe.wait_ge(casts_ready, 3 + FIRST)
            pe.wait_ge(hbias_ready, 1 + FIRST)

            with pe.Fori(0, B) as b:
                norm_sums(slot(stream, b), 0, b)
                pe.wait_ge(ln_ready, b * 2 + 1 + FIRST)
                for r in range(2):
                    pe.wait_ge(q0_ready, b * 2 + r + FIRST)
                    for i in range(2):
                        c = 2 * r + i
                        last = mm(QK0[:, i * T:(i + 1) * T], hw[:, A_Q + c * P:A_Q + (c + 1) * P], xn[:, :],
                                  start=True, stop=True)
                    last.then_inc(q0_done, 1)
                    pe.wait_ge(k0_ready, b * 2 + r + FIRST)
                    for i in range(2):
                        c = 2 * r + i
                        last = mm(QK1[:, i * T:(i + 1) * T], hw[:, A_K + c * P:A_K + (c + 1) * P], xn[:, :],
                                  start=True, stop=True)
                    last.then_inc(k0_done, 1)
                    if r == 0:
                        for t in range(TQ):
                            last = mm(NV[:, t * P:(t + 1) * P], xn[:, t * P:(t + 1) * P], hw[:, A_V:A_V + P],
                                      start=True, stop=True)
                        last.then_inc(v0_done, 1)
                pe.wait_ge(q0_ready, b * 2 + 2 + FIRST)
                pe.wait_ge(k0_ready, b * 2 + 2 + FIRST)

                def scores0(h):
                    c, s = h // HPC0, STRIP * (h % HPC0)
                    sc = (S0, S1)[h % 2]
                    if h >= 2:
                        pe.wait_ge(p0_ready, b * H + h - 1 + FIRST)
                    if h < 8:
                        mm(sc[:, 0:S0W], ident, toep[:, h * S0W:(h + 1) * S0W], start=True, stop=False)
                    else:
                        mm(sc[:, 0:S0W], identb[:, :], causalb[:, :], start=True, stop=False)
                    mm(sc[:, 0:P], qh[s:s + STRIP, c, 0:P], kh[s:s + STRIP, c, 0:P], start=False, stop=False)
                    mm(sc[:, P:S0W], qh[s:s + STRIP, c, P:T], kh[s:s + STRIP, c, :],
                       start=False, stop=True).then_inc(s0_done, 1)

                def transposes0(h):
                    tb = (TT, QK0)[h % 2]
                    pe.wait_ge(p0_ready, b * H + h + 1 + FIRST)
                    if h >= 2:
                        pe.wait_ge(pt0_ready, b * H + h - 1 + FIRST)
                    for i in range(3):
                        last = nc.tensor.transpose(tb[:, i * P:(i + 1) * P], prob0[:, h % 2, i * P:(i + 1) * P], ident)
                    last.then_inc(t0_done, 1)

                def values0(h):
                    if h == 0:
                        pe.wait_ge(v0_ready, b + 1 + FIRST)
                        pe.wait_ge(ao0_ready, b + FIRST)
                    pe.wait_ge(pt0_ready, b * H + h + 1 + FIRST)
                    o = OO[:, 0:TQ * H * (HD0 + 1)].rearrange("p (t h e) -> p t h e", t=TQ, h=H)
                    mm(o[:, 0, h, :], pt0[:, h % 2, 0:P], v0[:, 0, h, :], start=True, stop=True)
                    mm(o[:, 1, h, :], pt0[:, h % 2, P:2 * P], v0[:, 0, h, :], start=True, stop=False)
                    mm(o[:, 1, h, :], pt0[:, h % 2, 2 * P:3 * P], v0[:, 1, h, :], start=False, stop=True)\
                        .then_inc(pv0_done, 1)

                for h in range(H + 2):
                    if h < H:
                        scores0(h)
                    if 1 <= h <= H:
                        transposes0(h - 1)
                    if h >= 2:
                        values0(h - 2)
                pe.wait_ge(ao0_ready, b + 1 + FIRST)
                for t in range(TQ):
                    last = nc.tensor.transpose(NV[:, t * P:(t + 1) * P], ao0[:, t, :], ident)
                last.then_inc(aot0_done, 1)
                pe.wait_ge(aot0_ready, b + 1 + FIRST)
                mm(FF[:, 0:T], hw[:, A_P:A_P + P], aot0[:, :], start=True, stop=True).then_inc(y0_done, 1)
                pe.wait_ge(x1_ready, b + 1 + FIRST)
                norm_sums(slot(skip, b), 1, b)

            def step(n0, n, s, p, k0, k1, k2):
                G = n * NCH + p
                if p == 0 and k0 and not k1:
                    pe.wait_ge(wa_in, n0 + 16)
                if k0:
                    w, qk = p * WCH, (QK0, QK1)[p % 2]
                    if p == 0:
                        pe.wait_ge(xs_ready, n + 1 + FIRST)
                    pe.wait_ge(sq_ready, G - 1 + FIRST)
                    for i in range(2):
                        last = mm(qk[:, i * T:(i + 1) * T], wa[:, w + i * P:w + (i + 1) * P], xs[:, :],
                                  start=True, stop=True)
                    last.then_inc(qk_done, 1)
                    pe.wait_ge(guard_ready, G + FIRST)
                    for t in range(TQ):
                        last = mm(NV[:, t * P:(t + 1) * P], xs[:, t * P:(t + 1) * P],
                                  wa[:, w + 2 * P:w + 3 * P], start=True, stop=True)
                    last.then_inc(v_done, 1)
                if k2 and p == 0:
                    pe.wait_ge(fh_ready, n - 1 + FIRST)
                    for j in range(FC):
                        last = mm(FF[:, 0:T], wf[:, F_2 + j * P:F_2 + (j + 1) * P], fh[:, j, :],
                                  start=(j == 0), stop=(j == FC - 1))
                    last.then_inc(w2_done, 1)
                if k1:
                    if p == 1:
                        pe.wait_ge(wf_in, n0 + 16)
                        pe.wait_ge(xnew_ready, n - 1 + FIRST)
                    if p in WO_AT:
                        c0, c1 = WO_AT[p]
                        pe.wait_ge(aot_ready, (n - 1) * NCH + c1 + FIRST)
                        for c in range(c0, c1):
                            last = mm(FF[:, 0:T], wf[:, F_O + c * P:F_O + (c + 1) * P], aot[:, c, :],
                                      start=(c == 0), stop=(c == NCH - 1))
                        if c1 == NCH:
                            last.then_inc(y_done, 1)
                if present(p, 3, k0, k1):
                    pe.wait_ge(p_ready, G - 2 + FIRST)
                    if present(p, 5, k0, k1):
                        pe.wait_ge(aot_ready, G - 4 + FIRST)
                    for t in range(TQ):
                        for i in range(HPC):
                            k = TQ * t + i
                            src = pa[:, (p - 3) % 2, i, :] if t == 0 else pb[:, (p - 3) % 2, i, WIN:KB]
                            last = nc.tensor.transpose(TT[:, k * P:(k + 1) * P], src, ident)
                    last.then_inc(t_done, 1)
                if k1 and p == 5:
                    pe.wait_ge(fdsq_ready, n + FIRST)
                    mm(FF[:, 0:T], mean_w[:, :], dsq[:, :], start=True, stop=True).then_inc(fvar_done, 1)
                if k1 and p == 6:
                    up(n, 1)
                if present(p, 2, k0, k1):
                    par = p % 2
                    pe.wait_ge(p_ready, G - 2 + FIRST)
                    pe.wait_ge(kr_ready, G - 1 + FIRST)
                    for sc in (S0, S1):
                        mm(sc[:, 0:2 * KB], identb[:, :], localb[:, :], start=True, stop=False)
                    for i, sc in enumerate((S0, S1)):
                        f = HD * i
                        mm(sc[:, 0:P], qkr[f:f + HD, par, 0:P], kr[f:f + HD, par, 0:P], start=False, stop=False)
                    for i, sc in enumerate((S0, S1)):
                        f = HD * i
                        last = mm(sc[:, KB:2 * KB], qkr[f:f + HD, par, P:T], kr[f:f + HD, par, P - WIN:T],
                                  start=False, stop=True)
                    last.then_inc(s_done, 1)
                if present(p, 3, k0, k1):
                    par, q4 = (p - 3) % 2, (p - 3) % 4
                    pe.wait_ge(pt_ready, G - 2 + FIRST)
                    pe.wait_ge(ptp_ready, G - 2 + FIRST)
                    pe.wait_ge(ao_ready, G - 3 + FIRST)
                    o = OO[:, 0:4 * (HD + 1)].rearrange("p (k e) -> p k e", e=HD + 1)
                    for i in range(HPC):
                        mm(o[:, HPC + i, :], pt[:, par, (2 + i) * P:(3 + i) * P], vs[:, q4, 1, i, :],
                           start=(i == 0), stop=False)
                        mm(o[0:WIN, HPC + i, :], ptp[:, par, i, :], vp[:, q4, i, :], start=False, stop=False)
                    for i in range(HPC):
                        last = mm(o[:, i, :], pt[:, par, i * P:(i + 1) * P], vs[:, q4, 0, i, :],
                                  start=False, stop=(i == HPC - 1))
                    last.then_inc(pv_done, 1)
                if k0:
                    pe.wait_ge(sq_ready, G + 1 + FIRST)
                    pe.wait_ge(v_ready, G + 1 + FIRST)
                    mm(NV[:, 0:T], blk, sq[:, T:2 * T], start=True, stop=True)
                    for t in range(TQ):
                        last = mm(NV[:, T + 2 * t:T + 2 * t + 2], sq[:, t * P:(t + 1) * P], cst[:, C_BLK:C_BLK + P:HD],
                                  start=True, stop=True)
                    last.then_inc(n_done, 1)
                if present(p, 4, k0, k1):
                    pe.wait_ge(ao_ready, G - 3 + FIRST)
                    if present(p, 3, k0, k1):
                        pe.wait_ge(pt_ready, G - 2 + FIRST)
                    else:
                        pe.wait_ge(aot_ready, G - 4 + FIRST)
                    for t in range(TQ):
                        last = nc.tensor.transpose(TT[:, t * P:(t + 1) * P], ao[:, p % 2, t, :], ident)
                    last.then_inc(aot_done, 1)
                if k1 and p == 4:
                    pe.wait_ge(xs2_ready, n + FIRST)
                    mm(FF[:, 0:T], mean_w[:, :], xs2[:, :], start=True, stop=True).then_inc(fmean_done, 1)
                if k1 and p == 5:
                    up(n, 0)
                if k1 and p == 6:
                    up(n, 2)

            def up(n, j):
                pe.wait_ge(fxn_ready, n + FIRST)
                if j:
                    pe.wait_ge(fval_ready, (n - 1) * FC + j + FIRST)
                for i in range(2):
                    w = F_1 + (2 * j + i) * P
                    last = mm(FF[:, i * T:(i + 1) * T], wf[:, w:w + P], xn[:, :], start=True, stop=True)
                last.then_inc(w1_done, 1)

            pipeline(pe, step)

        @block.vector
        def _(dve):
            v = nc.vector
            for own in (setup_ready, casts_ready, hbias_ready, dev_ready, ln_ready, k0_ready, v0_ready,
                        max0_ready, pt0_ready, rec0_ready, ao0_ready, x1_ready, tables_ready, xs_ready, v_ready,
                        qkc_ready, qkx_ready, guard_ready, max_ready, nb_ready, ptp_ready, rec_ready, ao_ready,
                        xm_ready, xs2_ready, fdev_ready, fnorm_ready, fxn_ready, fval_ready, fh_ready,
                        xnew_ready, total_ready):
                dve.sem_inc(own, FIRST)
            v.memset(mean_w[:, :], 1.0 / D)
            v.memset(eps[:, :], EPS)
            v.memset(v0[:, :, :, :], 1.0)
            v.memset(vs[:, :, :, :, :], 1.0)
            v.memset(vp[:, :, :, :], 1.0)
            v.memset(xs[:, :], 0.0)
            v.memset(xs2[:, :], 0.0).then_inc(setup_ready, 1)
            dve.wait_ge(setup_ready, 1 + FIRST)
            dve.wait_ge(consts_in, 16)
            v.tensor_copy(identb[:, :], ident).then_inc(casts_ready, 1)
            v.tensor_copy(causalb[:, :], cst[:, C_CAUSAL:C_CAUSAL + S0W]).then_inc(casts_ready, 1)
            v.tensor_copy(localb[:, :], cst[:, C_LOCAL:C_LOCAL + 2 * KB]).then_inc(casts_ready, 1)
            dve.wait_ge(hope_in, 48)
            v.tensor_scalar(hbias[:, 0:4], hv[:, V_BQ:V_BQ + 4], HD0 ** -0.5, cst[:, C_ONE:C_ONE + 1],
                            ALU.mult, ALU.add)
            v.tensor_copy(hbias[:, 4:6], hv[:, V_BK:V_BK + 2])
            dve.wait_ge(pos_done, 1 + FIRST)
            v.tensor_tensor(hbias[:, 6:8], OO[:, 0:2], hv[:, V_BK + 2:V_BK + 4], ALU.add).then_inc(hbias_ready, 1)
            dve.wait_ge(hbias_ready, 1 + FIRST)

            def norm(src, dst, k, b):
                dve.wait_ge(mean_done, b * 2 + k + 1 + FIRST)
                dve.wait_ge(ln_ready, b * 2 + k + FIRST)
                v.tensor_tensor(dev[:, :], src, FF[:, 0:T], ALU.subtract).then_inc(dev_ready, 1)
                dve.wait_ge(rstd_ready, b * 2 + k + 1 + FIRST)
                v.tensor_tensor(dst, dev[:, :], rstd[:, :], ALU.mult).then_inc(ln_ready, 1)

            with dve.Fori(0, B) as b:
                norm(slot(stream, b), xn[:, :], 0, b)

                def k_evac(r):
                    dve.wait_ge(k0_done, b * 2 + r + 1 + FIRST)
                    for i in range(2):
                        c = 2 * r + i
                        last = v.tensor_scalar(kh[:, c, :], QK1[:, i * T:(i + 1) * T], hbias[:, 4 + c:5 + c], None, ALU.add)
                    last.then_inc(k0_ready, 1)

                k_evac(0)
                dve.wait_ge(v0_done, b + 1 + FIRST)
                v.tensor_copy(v0[:, :, :, 0:HD0], NV[:, 0:T].rearrange("p (t h e) -> p t h e", t=TQ, h=H))\
                    .then_inc(v0_ready, 1)
                k_evac(1)

                def maxima(h):
                    sc = (S0, S1)[h % 2]
                    dve.wait_ge(s0_done, b * H + h + 1 + FIRST)
                    v.tensor_reduce(nmax0[:, h, 0:1], sc[:, 0:P], AX, ALU.max, negate=True)
                    v.tensor_reduce(nmax0[:, h, 1:2], sc[:, P:S0W], AX, ALU.max, negate=True)\
                        .then_inc(max0_ready, 1)

                def pt_evac(h):
                    dve.wait_ge(t0_done, b * H + h + 1 + FIRST)
                    if h >= 2:
                        dve.wait_ge(pv0_done, b * H + h - 1 + FIRST)
                    v.tensor_copy(pt0[:, h % 2, :], (TT, QK0)[h % 2][:, 0:S0W]).then_inc(pt0_ready, 1)

                for h in range(H + 1):
                    if h < H:
                        maxima(h)
                    if h >= 1:
                        pt_evac(h - 1)
                dve.wait_ge(pv0_done, b * H + H + FIRST)
                o = OO[:, 0:TQ * H * (HD0 + 1)].rearrange("p (k e) -> p k e", e=HD0 + 1)
                v.reciprocal(rec0[:, :], o[:, :, HD0]).then_inc(rec0_ready, 1)
                dve.wait_ge(rec0_ready, b + 1 + FIRST)
                v.tensor_tensor(ao0[:, :, :].rearrange("p t (h e) -> p (t h) e", e=HD0), o[:, :, 0:HD0],
                                rec0[:, :].unsqueeze(2).to_broadcast([P, TQ * H, HD0]), ALU.mult)\
                    .then_inc(ao0_ready, 1)
                dve.wait_ge(y0_done, b + 1 + FIRST)
                v.scalar_tensor_tensor(slot(skip, b), FF[:, 0:T], hv[:, V_BP:V_BP + 1], slot(stream, b),
                                       ALU.add, ALU.add).then_inc(x1_ready, 1)
                norm(slot(skip, b), slot(stream, b), 1, b)

            def before_layer(l):
                dve.wait_ge(wa_in, l * 16 + 16)
                sc = NCH * WCH
                dve.wait_ge(qks_ready, l * (B * NCH) + FIRST)
                for i in range(2):
                    v.tensor_scalar(cosw[:, i * T:(i + 1) * T], cst[:, C_COS + i * T:C_COS + (i + 1) * T],
                                    wa[:, sc + 2 * i:sc + 2 * i + 1], None, ALU.mult)
                for i in range(2):
                    last = v.tensor_scalar(sinw[:, i * T:(i + 1) * T], cst[:, C_SIN + i * T:C_SIN + (i + 1) * T],
                                           wa[:, sc + 2 * i + 1:sc + 2 * i + 2], None, ALU.mult)
                last.then_inc(tables_ready, 1)
                dve.wait_ge(tables_ready, l + 1 + FIRST)

            def step(n0, n, s, p, k0, k1, k2):
                G = n * NCH + p
                if k0 and p == 0:
                    dve.wait_ge(v_done, G + FIRST)
                    dve.wait_ge(xnew_ready, n0 + FIRST)
                    src = slot(stream, s)
                    v.tensor_copy(xs[0:HD, :], src[0:HD, :])
                    v.tensor_copy(xs[HD:P, 1:T], src[HD:P, 0:T - 1]).then_inc(xs_ready, 1)
                if present(p, 1, k0, k1):
                    dve.wait_ge(n_done, G + FIRST)
                    dve.wait_ge(log2_ready, G - 1 + FIRST)
                    v.tensor_scalar(ng[:, :], NV[:, 0:T + 4], NORM_GUARD, None, ALU.max).then_inc(guard_ready, 1)
                if k1 and p == 5:
                    dve.wait_ge(fmean_done, n + FIRST)
                    v.tensor_tensor(dev[:, :], xs2[:, :], FF[:, 0:T], ALU.subtract).then_inc(fdev_ready, 1)
                if k1 and p == 6:
                    value(n, 0)
                if k1 and p == 7:
                    value(n, 2)
                if k0:
                    dve.wait_ge(qk_done, G + 1 + FIRST)
                    if p >= 2 or k1:
                        dve.wait_ge(qkr_ready, G - 1 + FIRST)
                    qk = (QK0, QK1)[p % 2]
                    v.tensor_tensor(qkc[:, p % 2, :], qk[:, :], cosw[:, :], ALU.mult).then_inc(qkc_ready, 1)
                    v.stream_shuffle(qkx[:, p % 2, :], qk[:, :], SWAP).then_inc(qkx_ready, 1)
                if present(p, 3, k0, k1):
                    dve.wait_ge(p_ready, G - 2 + FIRST)
                    if present(p, 5, k0, k1):
                        dve.wait_ge(pv_done, G - 4 + FIRST)
                    v.transpose(ptp[:, (p - 3) % 2, :, :], pb[0:WIN, (p - 3) % 2, :, 0:WIN]).then_inc(ptp_ready, 1)
                if k2 and p == 0:
                    dve.wait_ge(w2_done, n - 1 + FIRST)
                    v.scalar_tensor_tensor(slot(stream, s - 2), FF[:, 0:T], wf[:, F_B2:F_B2 + 1], xm[:, :],
                                           ALU.add, ALU.add).then_inc(xnew_ready, 1)
                if k0:
                    dve.wait_ge(v_done, G + 1 + FIRST)
                    nv = NV[:, 0:T].rearrange("p (t i e) -> p t i e", t=TQ, i=HPC)
                    v.tensor_copy(vs[:, p % 4, :, :, 0:HD], nv)
                    v.tensor_copy(vp[:, p % 4, :, 0:HD], nv[P - WIN:P, 0, :, :]).then_inc(v_ready, 1)
                if k1 and p == 4:
                    dve.wait_ge(y_done, n + FIRST)
                    dve.wait_ge(xnew_ready, n - 1 + FIRST)
                    v.tensor_tensor(xm[:, :], FF[:, 0:T], slot(stream, s - 1), ALU.add).then_inc(xm_ready, 1)
                    dve.wait_ge(xm_ready, n + FIRST)
                    v.tensor_copy(xs2[0:HD, :], xm[0:HD, :])
                    v.tensor_copy(xs2[HD:P, 1:T], xm[HD:P, 0:T - 1]).then_inc(xs2_ready, 1)
                if k1 and p == 5:
                    dve.wait_ge(frstd_ready, n + FIRST)
                    v.scalar_tensor_tensor(dev[:, :], dev[:, :], wf[:, F_G:F_G + 1], rstd[:, :], ALU.mult, ALU.mult)\
                        .then_inc(fnorm_ready, 1)
                    dve.wait_ge(fnorm_ready, n + FIRST)
                    v.tensor_scalar(xn[:, :], dev[:, :], wf[:, F_B:F_B + 1], None, ALU.add)\
                        .then_inc(fxn_ready, 1)
                if k1 and p == 6:
                    value(n, 1)
                if present(p, 2, k0, k1):
                    par = p % 2
                    dve.wait_ge(s_done, G - 1 + FIRST)
                    dve.wait_ge(nb_ready, G - 2 + FIRST)
                    v.tensor_reduce(nm[:, 0:2], S0[:, 0:2 * KB].rearrange("p (i j) -> p i j", j=KB), AX, ALU.max,
                                    negate=True)
                    v.tensor_reduce(nm[:, 2:4], S1[:, 0:2 * KB].rearrange("p (i j) -> p i j", j=KB), AX, ALU.max,
                                    negate=True).then_inc(max_ready, 1)
                    dve.wait_ge(max_ready, G - 1 + FIRST)
                    dve.wait_ge(rn_ready, G - 1 + FIRST)
                    if present(p, 4, k0, k1):
                        dve.wait_ge(p_ready, G - 3 + FIRST)
                    v.tensor_tensor(nb[:, par, :].rearrange("p (i t) -> p i t", t=TQ),
                                    nm[:, :].rearrange("p (i t) -> p i t", t=TQ),
                                    rn[:, par, T:T + 4].rearrange("p (t i) -> p i t", i=HPC), ALU.mult)\
                        .then_inc(nb_ready, 1)
                if present(p, 3, k0, k1):
                    dve.wait_ge(pv_done, G - 2 + FIRST)
                    if present(p, 5, k0, k1):
                        dve.wait_ge(aot_done, G - 4 + FIRST)
                    o = OO[:, 0:4 * (HD + 1)].rearrange("p (k e) -> p k e", e=HD + 1)
                    dve.wait_ge(ao_ready, G - 3 + FIRST)
                    v.reciprocal(rec[:, :], o[:, :, HD]).then_inc(rec_ready, 1)
                    dve.wait_ge(rec_ready, G - 2 + FIRST)
                    v.tensor_tensor(ao[:, (p - 3) % 2, :, :].rearrange("p t (i e) -> p (t i) e", e=HD), o[:, :, 0:HD],
                                    rec[:, :].unsqueeze(2).to_broadcast([P, 4, HD]), ALU.mult)\
                        .then_inc(ao_ready, 1)
                if k1 and p == 7:
                    dve.wait_ge(fact_ready, n + FIRST)
                    dve.wait_ge(fval_ready, n * FC + FIRST)
                    v.tensor_tensor(fh[:, :, :], fval[:, :, :], fact[:, :, :], ALU.mult).then_inc(fh_ready, 1)

            def value(n, j):
                dve.wait_ge(fgate_ready, (n - 1) * FC + j + 1 + FIRST)
                v.tensor_scalar(fval[:, j, :], FF[:, 0:T], wf[:, F_B1 + 2 * j:F_B1 + 2 * j + 1], None, ALU.add)\
                    .then_inc(fval_ready, 1)

            dve.wait_ge(ln_ready, 2 * B + FIRST)
            pipeline(dve, step, before_layer)
            dve.wait_ge(xnew_ready, L * B + FIRST)
            for g in range(4):
                w = B * T // 4
                v.tensor_tensor(total[:, g, :], stream[:, g * w:(g + 1) * w], skip[:, g * w:(g + 1) * w], ALU.add)\
                    .then_inc(total_ready, 1)

        @block.scalar
        def _(act):
            a = nc.scalar.activation
            for own in (dsq_ready, log_ready, rstd_ready, q0_ready, p0_ready, aot0_ready, sq_ready, log2_ready,
                        rn_ready, p_ready, pt_ready, aot_ready, fdsq_ready, flog_ready, frstd_ready, fgate_ready,
                        fact_ready):
                act.sem_inc(own, FIRST)
            nc.scalar.preload_act_table_set("natural_log_exp_and_others")
            act.wait_ge(setup_ready, 1 + FIRST)
            act.wait_ge(hbias_ready, 1 + FIRST)

            def norm(k, b):
                act.wait_ge(dev_ready, b * 2 + k + 1 + FIRST)
                a(dsq[:, :], dev[:, :], ACT.Square).then_inc(dsq_ready, 1)
                act.wait_ge(var_done, b * 2 + k + 1 + FIRST)
                a(logv[:, :], FF[:, 0:T], ACT.Ln, bias=eps[:, 0:1]).then_inc(log_ready, 1)
                act.wait_ge(log_ready, b * 2 + k + 1 + FIRST)
                a(rstd[:, :], logv[:, :], ACT.Exp, scale=-0.5).then_inc(rstd_ready, 1)

            with act.Fori(0, B) as b:
                norm(0, b)
                for r in range(2):
                    act.wait_ge(q0_done, b * 2 + r + 1 + FIRST)
                    for i in range(2):
                        c = 2 * r + i
                        last = a(qh[:, c, :], QK0[:, i * T:(i + 1) * T], ACT.Identity, bias=hbias[:, c:c + 1],
                                 scale=HD0 ** -0.5)
                    last.then_inc(q0_ready, 1)
                for h in range(H):
                    sc = (S0, S1)[h % 2]
                    act.wait_ge(max0_ready, b * H + h + 1 + FIRST)
                    if h >= 2:
                        act.wait_ge(t0_done, b * H + h - 1 + FIRST)
                    a(prob0[:, h % 2, 0:P], sc[:, 0:P], ACT.Exp, bias=nmax0[:, h, 0:1])
                    a(prob0[:, h % 2, P:S0W], sc[:, P:S0W], ACT.Exp, bias=nmax0[:, h, 1:2]).then_inc(p0_ready, 1)
                act.wait_ge(aot0_done, b + 1 + FIRST)
                a(aot0[:, :], NV[:, 0:T], ACT.Identity, bias=hv[:, V_BV:V_BV + 1]).then_inc(aot0_ready, 1)
                norm(1, b)

            def step(n0, n, s, p, k0, k1, k2):
                G = n * NCH + p
                if present(p, 1, k0, k1):
                    act.wait_ge(guard_ready, G + FIRST)
                    act.wait_ge(rn_ready, G - 1 + FIRST)
                    a(lg[:, :], ng[:, :], ACT.Ln).then_inc(log2_ready, 1)
                    act.wait_ge(log2_ready, G + FIRST)
                    if present(p, 3, k0, k1):
                        act.wait_ge(kr_ready, G - 2 + FIRST)
                        act.wait_ge(p_ready, G - 2 + FIRST)
                    a(rn[:, (p - 1) % 2, :], lg[:, :], ACT.Exp, scale=-0.5).then_inc(rn_ready, 1)
                if k1 and p == 5:
                    act.wait_ge(fdev_ready, n + FIRST)
                    a(dsq[:, :], dev[:, :], ACT.Square).then_inc(fdsq_ready, 1)
                if k1 and p == 6:
                    gate(n, 0)
                if k1 and p == 7:
                    gate(n, 2)
                if present(p, 3, k0, k1):
                    act.wait_ge(t_done, G - 2 + FIRST)
                    if present(p, 5, k0, k1):
                        act.wait_ge(pv_done, G - 4 + FIRST)
                    a(pt[:, (p - 3) % 2, :], TT[:, :], ACT.Copy).then_inc(pt_ready, 1)
                if k0:
                    act.wait_ge(qkx_ready, G + 1 + FIRST)
                    act.wait_ge(n_done, G + FIRST)
                    a(sq[:, :], (QK0, QK1)[p % 2][:, :], ACT.Square).then_inc(sq_ready, 1)
                if k1 and p == 5:
                    act.wait_ge(fvar_done, n + FIRST)
                    a(logv[:, :], FF[:, 0:T], ACT.Ln, bias=eps[:, 0:1]).then_inc(flog_ready, 1)
                    act.wait_ge(flog_ready, n + FIRST)
                    a(rstd[:, :], logv[:, :], ACT.Exp, scale=-0.5).then_inc(frstd_ready, 1)
                if k1 and p == 6:
                    gate(n, 1)
                if k1 and p == 7:
                    act.wait_ge(fgate_ready, n * FC + FIRST)
                    a(fact[:, :, :], fgate[:, :, :], ACT.Gelu).then_inc(fact_ready, 1)
                    nc.scalar.preload_act_table_set("natural_log_exp_and_others")
                if present(p, 2, k0, k1):
                    par = p % 2
                    act.wait_ge(nb_ready, G - 1 + FIRST)
                    if present(p, 4, k0, k1):
                        act.wait_ge(t_done, G - 3 + FIRST)
                        act.wait_ge(ptp_ready, G - 3 + FIRST)
                    for i, sc in enumerate((S0, S1)):
                        k, r = TQ * i, T + i
                        a(pa[:, par, i, :], sc[:, 0:P], ACT.Exp, bias=nb[:, par, k:k + 1],
                          scale=rn[:, par, r:r + 1])
                        k, r = k + 1, r + HPC
                        last = a(pb[:, par, i, :], sc[:, KB:2 * KB], ACT.Exp, bias=nb[:, par, k:k + 1],
                                 scale=rn[:, par, r:r + 1])
                    last.then_inc(p_ready, 1)
                if present(p, 4, k0, k1):
                    c = (p - 4) % NCH
                    act.wait_ge(aot_done, G - 3 + FIRST)
                    if c == 0 and k1:
                        act.wait_ge(y_done, n + FIRST)
                    a(aot[:, c, :], TT[:, 0:T], ACT.Copy).then_inc(aot_ready, 1)

            def gate(n, j):
                act.wait_ge(w1_done, (n - 1) * FC + j + 1 + FIRST)
                b1 = F_B1 + 2 * j + 1
                a(fgate[:, j, :], FF[:, T:2 * T], ACT.Identity, bias=wf[:, b1:b1 + 1]).then_inc(fgate_ready, 1)

            pipeline(act, step)

        @block.gpsimd
        def _(pool):
            g = nc.gpsimd
            for own in (qks_ready, qkr_ready, kr_ready):
                pool.sem_inc(own, FIRST)

            def step(n0, n, s, p, k0, k1, k2):
                G = n * NCH + p
                if present(p, 1, k0, k1):
                    par = (p - 1) % 2
                    pool.wait_ge(qkr_ready, G + FIRST)
                    pool.wait_ge(rn_ready, G + FIRST)
                    if present(p, 3, k0, k1):
                        pool.wait_ge(s_done, G - 2 + FIRST)
                    g.tensor_tensor(kr[:, par, :], qkr[:, par, T:2 * T], rn[:, par, 0:T], ALU.mult)\
                        .then_inc(kr_ready, 1)
                if k0:
                    par = p % 2
                    pool.wait_ge(qkx_ready, G + 1 + FIRST)
                    g.tensor_tensor(qks[:, par, :], qkx[:, par, :], sinw[:, :], ALU.mult).then_inc(qks_ready, 1)
                    pool.wait_ge(qks_ready, G + 1 + FIRST)
                    if p >= 2 or k1:
                        pool.wait_ge(s_done, G - 1 + FIRST)
                    g.tensor_tensor(qkr[:, par, :], qkc[:, par, :], qks[:, par, :], ALU.add).then_inc(qkr_ready, 1)

            pipeline(pool, step)


def constants():
    c = np.zeros((P, C_N), np.float32)
    c[:, C_ID:C_ID + P] = np.eye(P, dtype=np.float32)
    i = np.arange(P)[:, None]
    ch = np.where(i >= np.arange(P)[None], 0.0, MASKED)
    cw = np.where(i + P >= np.arange(T)[None], 0.0, MASKED)
    c[:, C_CAUSAL:C_CAUSAL + S0W] = np.concatenate([ch, cw], 1)
    d0 = i - np.arange(P)[None]
    d1 = i + WIN - np.arange(KB)[None]
    m0, m1 = (np.where((d >= 0) & (d <= WIN), 0.0, MASKED) for d in (d0, d1))
    none = np.full((P, KB - P), MASKED)
    c[:, C_LOCAL:C_LOCAL + 2 * KB] = np.concatenate([m0, none, m1], 1)
    half = np.arange(0, HD, 2, dtype=np.float32)
    inv_freq = (np.float32(1.0) / np.float32(10000.0) ** (half / np.float32(HD))).astype(np.float32)
    t = np.arange(T, dtype=np.float32)
    fr = t[:, None] * inv_freq[None]
    fr = np.concatenate([fr, fr], 1)
    base = ((half + np.float32(0.4 * HD)) / np.float32(1.4 * HD)).astype(np.float32)
    scale = base[None].astype(np.float64) ** ((t - T // 2) / np.float32(WIN // 2))[:, None].astype(np.float64)
    scale = np.concatenate([scale, scale], 1)
    cos, sin = np.cos(fr.astype(np.float64)), np.sin(fr.astype(np.float64))
    sign = np.where(np.arange(HD) < HD // 2, -1.0, 1.0)[None]
    for k, sc in enumerate((8.0 * scale, 1.0 / scale)):
        at = C_COS + k * T
        c[:, at:at + T] = np.tile((cos * sc).T[ORDER], (2, 1))
        at = C_SIN + k * T
        c[:, at:at + T] = np.tile((sin * sign * sc).T[ORDER], (2, 1))
    c[:, C_BLK:C_BLK + P] = np.kron(np.eye(2), np.ones((HD, HD)))
    rows = np.arange(HPC0) * STRIP + HD0
    c[rows, C_ONE] = 1.0
    for ck in range(2):
        for s in range(HPC0):
            hh = HPC0 * ck + s
            c[8 * hh:8 * hh + 8, C_POS + ck * P + s * STRIP + HD0] = 1.0
    dim = D // 2
    fq = (1.0 / 1250 ** (np.arange(dim, dtype=np.float64) / dim))[:dim - D // 4].astype(np.float32)
    dd = np.arange(-(T - 1), T, dtype=np.float32)
    th = dd[:, None] * fq[None]
    pv = np.cos(th).astype(np.float32) + np.sin(th).astype(np.float32)
    ph = pv.reshape(2 * T - 1, 8, 4).sum(-1)
    tp = np.zeros((P, 8, S0W), np.float32)
    for h in range(8):
        a0 = np.where(ch == 0, ph[i - np.arange(P)[None] + T - 1, h], MASKED)
        a1 = np.where(cw == 0, ph[i + P - np.arange(T)[None] + T - 1, h], MASKED)
        tp[:, h] = np.concatenate([a0, a1], 1)
    return c, tp.reshape(P, 8 * S0W)


def kernel(**inputs):
    import concourse.bacc as bacc
    from concourse.bass_utils import run_bass_kernel_spmd

    g = {k: np.asarray(v) for k, v in inputs.items()}
    f = np.float32
    consts, toeplitz = constants()
    x = np.ascontiguousarray(g["L0_attn_x"].transpose(0, 2, 1))
    wqkv = g["L0_attn_w_qkv"].reshape(3, NC0, HPC0, HD0, D)
    bqkv = g["L0_attn_b_qkv"].reshape(3, NC0, HPC0, HD0)
    hope_w = np.zeros((P, A_N), f)
    hope_v = np.zeros((P, V_N), f)
    for at, bt, k in ((A_Q, V_BQ, 0), (A_K, V_BK, 1)):
        w = np.zeros((NC0, HPC0, STRIP, D), f)
        w[:, :, :HD0] = wqkv[k]
        hope_w[:, at:at + NC0 * P] = w.reshape(NC0 * P, D).T
        bb = np.zeros((NC0, HPC0, STRIP), f)
        bb[:, :, :HD0] = bqkv[k]
        hope_v[:, bt:bt + NC0] = bb.reshape(NC0, P).T
    hope_w[:, A_V:A_V + D] = g["L0_attn_w_qkv"][2 * D:].T
    hope_w[:, A_P:A_P + D] = g["L0_attn_w_proj"].T
    hope_v[:, V_BV] = g["L0_attn_b_qkv"][2 * D:]
    hope_v[:, V_BP] = g["L0_attn_b_proj"]
    hope_v[:64, V_POS] = g["L0_attn_pos_independent"].reshape(64)
    order = np.array(ORDER)
    partner = (order + HD // 2) % HD
    w = g["L0_ffn_Wqkv"].reshape(L, D, 3, NCH, HPC, HD)
    attn_w = np.zeros((L, P, WA_N), f)
    parts = np.stack([w[:, :, 0][..., order], w[:, :, 1][..., order], w[:, :, 2]], 3)
    attn_w[:, :, :NCH * WCH] = parts.reshape(L, D, NCH * WCH)
    for i, (nm, at) in enumerate((("q", order), ("q", partner), ("k", order), ("k", partner))):
        sc = g[f"L0_ffn_{nm}_scale"][:, at]
        attn_w[:, :HD, NCH * WCH + i] = sc
        attn_w[:, HD:, NCH * WCH + i] = sc
    ffn_w = np.zeros((L, P, WF_N), f)
    ffn_w[:, :, F_O:F_O + NCH * P] = g["L0_ffn_Wo"].reshape(L, NCH, P, D).transpose(0, 2, 1, 3).reshape(L, P, NCH * D)
    w1 = np.zeros((L, D, FC, 2, P), f)
    b1 = np.zeros((L, FC, 2, P), f)
    w2 = np.zeros((L, FC * P, D), f)
    w2[:, :FI] = g["L0_ffn_W2"]
    for j in range(FC):
        e = min(P, FI - j * P)
        for i in range(2):
            at = i * FI + j * P
            w1[:, :, j, i, :e] = g["L0_ffn_W1"][:, :, at:at + e]
            b1[:, j, i, :e] = g["L0_ffn_b1"][:, at:at + e]
    ffn_w[:, :, F_1:F_1 + 2 * FC * P] = w1.reshape(L, D, 2 * FC * P)
    ffn_w[:, :, F_2:F_2 + FC * P] = w2.reshape(L, FC, P, D).transpose(0, 2, 1, 3).reshape(L, P, FC * D)
    ffn_w[:, :, F_G] = g["L0_ffn_ln_g"]
    ffn_w[:, :, F_B] = g["L0_ffn_ln_b"]
    ffn_w[:, :, F_B1:F_B1 + 2 * FC] = b1.reshape(L, 2 * FC, P).transpose(0, 2, 1)
    ffn_w[:, :, F_B2] = g["L0_ffn_b2"]

    nc = bacc.Bacc("TRN2", target_bir_lowering=False, num_devices=1)
    arrays, args = {}, []
    for name, arr in (("x", x), ("consts", consts), ("toeplitz", toeplitz), ("hope_w", hope_w), ("hope_v", hope_v),
                      ("attn_w", attn_w), ("ffn_w", ffn_w)):
        arr = np.ascontiguousarray(arr)
        arrays[f"in_{name}"] = arr
        args.append(nc.dram_tensor(f"in_{name}", arr.shape, mybir.dt.from_np(arr.dtype), kind="ExternalInput").ap())
    args.append(nc.dram_tensor("out_y", (B, D, T), F32, kind="ExternalOutput").ap())
    sequence_kernel(nc, *args)
    r = run_bass_kernel_spmd(nc, [arrays], core_ids=[0])
    return np.ascontiguousarray(r.results[0]["out_y"].transpose(0, 2, 1))
```

```python
from contextlib import ExitStack

import concourse.bass as bass
import numpy as np
from concourse import mybir

F32 = mybir.dt.float32
BF16 = mybir.dt.bfloat16
F32R = mybir.dt.float32r
ALU = mybir.AluOpType
ACT = mybir.ActivationFunctionType
AX = mybir.AxisListType.X

P = 128
B, T, D = 16, 256, 128
TQ = T // P
H = 16
HD0 = D // H
STRIP = 32
HPC0 = P // STRIP
NC0 = H // HPC0
HD = 64
HPC = P // HD
NCH = H // HPC
L = 6
WIN = 32
FI = 341
FC = 3
KB = P + WIN
S0W = 3 * P
EPS = 1e-5
MASKED = -1e30
NORM_GUARD = 1e-24

SWAP = [(r + 16) % 32 for r in range(32)]
ORDER = [16 * a + r if r < 16 else HD // 2 + 16 * a + r - 16 for a in range(2) for r in range(32)]

C_ID, C_CAUSAL, C_LOCAL, C_COS, C_SIN, C_BLK, C_ONE, C_POS = 0, 128, 512, 832, 1344, 1856, 1984, 1985
C_N = C_POS + 2 * P
A_Q, A_K, A_V, A_P, A_N = 0, 512, 1024, 1152, 1280
V_BQ, V_BK, V_BV, V_BP, V_POS, V_N = 0, 4, 8, 9, 10, 11
WCH = 3 * P
WA_N = NCH * WCH + 4
F_O = 0
F_1 = F_O + NCH * P
F_G = F_1 + 2 * FC * P
F_B = F_G + 1
F_B1 = F_B + 1
F_2 = F_B1 + 2 * FC
F_B2 = F_2 + FC * P
WF_N = F_B2 + 1


def sequence_kernel(nc, x, consts, toeplitz, hope_w, hope_v, attn_w, ffn_w, out):
    with ExitStack() as ctx:
        def sb(name, shape, dt=F32):
            return ctx.enter_context(nc.sbuf_tensor(name, shape, dt))

        def sem(name):
            return ctx.enter_context(nc.semaphore(name))

        stream = sb("stream", [P, B * T])
        skip = sb("skip", [P, B * T])
        cst = sb("cst", [P, C_N])
        hv = sb("hv", [P, V_N])
        wa = sb("wa", [P, WA_N])
        wf = sb("wf", [P, WF_N])
        identb = sb("identb", [P, P], BF16)
        causalb = sb("causalb", [P, S0W], BF16)
        localb = sb("localb", [P, 2 * KB], BF16)
        mean_w = sb("mean_w", [P, P])
        eps = sb("eps", [P, 1])
        dev = sb("dev", [P, T])
        dsq = sb("dsq", [P, T])
        logv = sb("logv", [P, T])
        rstd = sb("rstd", [P, T])
        xn = sb("xn", [P, T])
        first = ExitStack()

        def sb0(name, shape, dt=F32):
            return first.enter_context(nc.sbuf_tensor(name, shape, dt))

        toep = sb0("toep", [P, 8 * S0W])
        th = sb0("th", [P, 8 * S0W], F32R)
        tr = sb0("tr", [P, 8 * S0W], F32R)
        identr = sb0("identr", [P, P], F32R)
        hw = sb0("hw", [P, A_N])
        hbias = sb0("hbias", [P, 8])
        qh = sb0("qh", [P, NC0, T])
        kh = sb0("kh", [P, NC0, T])
        v0 = sb0("v0", [P, TQ, H, HD0 + 1])
        nmax0 = sb0("nmax0", [P, H, TQ])
        prob0 = sb0("prob0", [P, 2, S0W])
        pt0 = sb0("pt0", [P, 2, S0W])
        rec0 = sb0("rec0", [P, TQ * H])
        ao0 = sb0("ao0", [P, TQ, D])
        aot0 = sb0("aot0", [P, T])
        first.close()
        wh = sb("wh", [P, NCH * 2 * P], F32R)
        wr = sb("wr", [P, NCH * 2 * P], F32R)
        wv = sb("wv", [P, NCH * P])
        xs = sb("xs", [P, 2, T])
        xh = sb("xh", [P, 2, T], F32R)
        xr = sb("xr", [P, 2, T], F32R)
        cosw = sb("cosw", [P, 2 * T])
        sinw = sb("sinw", [P, 2 * T])
        sq = sb("sq", [P, 2 * T])
        qkc = sb("qkc", [P, 2, 2 * T])
        qkx = sb("qkx", [P, 2, 2 * T])
        qks = sb("qks", [P, 2, 2 * T])
        qkr = sb("qkr", [P, 2, 2 * T])
        kr = sb("kr", [P, 2, T])
        ng = sb("ng", [P, T + 4])
        lg = sb("lg", [P, T + 4])
        rn = sb("rn", [P, 2, T + 4])
        nm = sb("nm", [P, 4])
        nb = sb("nb", [P, 2, 4])
        pa = sb("pa", [P, 2, HPC, P])
        pb = sb("pb", [P, 2, HPC, KB])
        pt = sb("pt", [P, 2, 4 * P])
        ptp = sb("ptp", [WIN, 2, HPC, WIN])
        vs = sb("vs", [P, NCH, TQ, HPC, HD + 1])
        vp = sb("vp", [WIN, NCH, HPC, HD + 1])
        rec = sb("rec", [P, 4])
        ao = sb("ao", [P, 2, TQ, P])
        aot = sb("aot", [P, NCH, T])
        w1h = sb("w1h", [P, 2 * FC * P], F32R)
        w1r = sb("w1r", [P, 2 * FC * P], F32R)
        nh = sb("nh", [P, T], F32R)
        nr = sb("nr", [P, T], F32R)
        xm = sb("xm", [P, T])
        xs2 = sb("xs2", [P, T])
        fval = sb("fval", [P, FC, T])
        fgate = sb("fgate", [P, FC, T])
        fact = sb("fact", [P, FC, T])
        fh = sb("fh", [P, FC, T])

        def bank(name):
            return ctx.enter_context(nc.psum_tensor(name, [P, 512], F32))

        QK0, QK1, NV, S0, S1, TT, OO, FF = [bank(n) for n in ("QK0", "QK1", "NV", "S0", "S1", "TT", "OO", "FF")]

        ident = cst[:, C_ID:C_ID + P]
        blk = cst[:, C_BLK:C_BLK + P]

        pos_done = sem("pos_done")
        mean_done = sem("mean_done")
        var_done = sem("var_done")
        q0_done = sem("q0_done")
        k0_done = sem("k0_done")
        v0_done = sem("v0_done")
        s0_done = sem("s0_done")
        t0_done = sem("t0_done")
        pv0_done = sem("pv0_done")
        aot0_done = sem("aot0_done")
        y0_done = sem("y0_done")
        qk_done = sem("qk_done")
        v_done = sem("v_done")
        s_done = sem("s_done")
        n_done = sem("n_done")
        pv_done = sem("pv_done")
        t_done = sem("t_done")
        aot_done = sem("aot_done")
        y_done = sem("y_done")
        fmean_done = sem("fmean_done")
        fvar_done = sem("fvar_done")
        w1_done = sem("w1_done")
        w2_done = sem("w2_done")
        setup_ready = sem("setup_ready")
        casts_ready = sem("casts_ready")
        hbias_ready = sem("hbias_ready")
        dev_ready = sem("dev_ready")
        ln_ready = sem("ln_ready")
        k0_ready = sem("k0_ready")
        v0_ready = sem("v0_ready")
        max0_ready = sem("max0_ready")
        pt0_ready = sem("pt0_ready")
        rec0_ready = sem("rec0_ready")
        ao0_ready = sem("ao0_ready")
        x1_ready = sem("x1_ready")
        tables_ready = sem("tables_ready")
        split_ready = sem("split_ready")
        high_ready = sem("high_ready")
        shift_ready = sem("shift_ready")
        xh_ready = sem("xh_ready")
        xs_ready = sem("xs_ready")
        v_ready = sem("v_ready")
        qkc_ready = sem("qkc_ready")
        qkx_ready = sem("qkx_ready")
        guard_ready = sem("guard_ready")
        max_ready = sem("max_ready")
        nb_ready = sem("nb_ready")
        ptp_ready = sem("ptp_ready")
        rec_ready = sem("rec_ready")
        ao_ready = sem("ao_ready")
        xm_ready = sem("xm_ready")
        xs2_ready = sem("xs2_ready")
        fdev_ready = sem("fdev_ready")
        fnorm_ready = sem("fnorm_ready")
        fxn_ready = sem("fxn_ready")
        nh_ready = sem("nh_ready")
        nr_ready = sem("nr_ready")
        w1h_ready = sem("w1h_ready")
        w1r_ready = sem("w1r_ready")
        fval_ready = sem("fval_ready")
        fh_ready = sem("fh_ready")
        xnew_ready = sem("xnew_ready")
        total_ready = sem("total_ready")
        dsq_ready = sem("dsq_ready")
        log_ready = sem("log_ready")
        rstd_ready = sem("rstd_ready")
        q0_ready = sem("q0_ready")
        p0_ready = sem("p0_ready")
        aot0_ready = sem("aot0_ready")
        sq_ready = sem("sq_ready")
        log2_ready = sem("log2_ready")
        rn_ready = sem("rn_ready")
        p_ready = sem("p_ready")
        pt_ready = sem("pt_ready")
        aot_ready = sem("aot_ready")
        fdsq_ready = sem("fdsq_ready")
        flog_ready = sem("flog_ready")
        frstd_ready = sem("frstd_ready")
        fgate_ready = sem("fgate_ready")
        fact_ready = sem("fact_ready")
        high0_ready = sem("high0_ready")
        bias0_ready = sem("bias0_ready")
        qks_ready = sem("qks_ready")
        qkr_ready = sem("qkr_ready")
        kr_ready = sem("kr_ready")
        sinw_ready = sem("sinw_ready")
        consts_in = sem("consts_in")
        hope_in = sem("hope_in")
        toep_in = sem("toep_in")
        x0_in = sem("x0_in")
        x_in = sem("x_in")
        wa_in = sem("wa_in")
        wo_in = sem("wo_in")
        w1_in = sem("w1_in")
        w2_in = sem("w2_in")
        out_in = sem("out_in")
        FIRST = 1

        block = ctx.enter_context(nc.Block())

        def slot(t, n):
            return t[:, bass.ds(n * T, T)]

        SLOT_V, SLOT_Q1, SLOT_OUT, SLOT_K1, SLOT_Y, SLOT_MEAN2, SLOT_VAR2 = 0, 1, 3, 3, 4, 5, 6
        SLOT_MEAN1, SLOT_VAR1, SLOT_Q0, SLOT_K0 = 8, 9, 11, 12

        def attention0(eng, prepare, body, finish):
            prepare()
            body(0, False, True)
            with eng.Fori(1, B - 1) as b:
                body(b, True, True)
            body(B - 1, True, False)
            finish()

        def present(p, lag, k0, k1):
            return k0 if p >= lag else k1

        def pipeline(eng, step):
            def sequence(l, s, par, k1, k2, role=None, more=True):
                if role == "first":
                    at = (0, B - 1, B - 2, 1)
                elif role == "second":
                    at = (1, 0, B - 1, 2)
                elif role == "last":
                    at = (B - 1, B - 2, B - 3, 0 if more else None)
                else:
                    at = (s, s - 1, s - 2, s + 1)
                for p in range(NCH):
                    step(l, l * B + s, at, p, True, k1, k2, role, par)

            def middle(l):
                with eng.Fori(1, B // 2 - 1) as h:
                    for par in range(2):
                        sequence(l, 2 * h + par, par, True, True)
                sequence(l, B - 2, 0, True, True)

            sequence(0, 0, 0, False, False, "first")
            sequence(0, 1, 1, True, False, "second")
            with eng.Fori(0, L - 1) as l:
                middle(l)
                sequence(l, B - 1, 1, True, True, "last")
                sequence(l + 1, 0, 0, True, True, "first")
                sequence(l + 1, 1, 1, True, True, "second")
            middle(L - 1)
            sequence(L - 1, B - 1, 1, True, True, "last", more=False)
            for p in range(NCH):
                step(L - 1, L * B, (None, B - 1, B - 2, None), p, False, True, True, None, 0)
            for p in range(6):
                step(L - 1, L * B + 1, (None, None, B - 1, None), p, False, False, True, None, 1)

        @block.sync
        def _(sp):
            def load_x(g):
                w = B // 4
                return sp.dma_start(stream[:, g * w * T:(g + 1) * w * T].rearrange("p (b t) -> p b t", t=T),
                                    x[g * w:(g + 1) * w].rearrange("b p t -> p b t"))

            load_x(0).then_inc(x0_in, 16)
            sp.dma_start(hv[:, :], hope_v).then_inc(hope_in, 16)
            sp.dma_start(hw[:, :], hope_w).then_inc(hope_in, 16)
            sp.dma_start(cst[:, :], consts).then_inc(consts_in, 16)
            sp.dma_start(toep[:, :], toeplitz).then_inc(toep_in, 16)
            for g in range(1, 4):
                load_x(g).then_inc(x_in, 16)
            sp.dma_start(wa[:, :], attn_w[0]).then_inc(wa_in, 16)
            sp.dma_start(wf[:, F_O:F_1], ffn_w[0, :, F_O:F_1]).then_inc(wo_in, 16)
            sp.dma_start(wf[:, F_1:F_2], ffn_w[0, :, F_1:F_2]).then_inc(w1_in, 16)
            sp.dma_start(wf[:, F_2:WF_N], ffn_w[0, :, F_2:WF_N]).then_inc(w2_in, 16)
            for l in range(1, L):
                sp.wait_ge(split_ready, l * NCH + FIRST)
                sp.wait_ge(tables_ready, l + FIRST)
                sp.wait_ge(sinw_ready, l + FIRST)
                sp.dma_start(wa[:, :], attn_w[l]).then_inc(wa_in, 16)
                sp.wait_ge(y_done, l * B + FIRST)
                sp.dma_start(wf[:, F_O:F_1], ffn_w[l, :, F_O:F_1]).then_inc(wo_in, 16)
                sp.wait_ge(w1_done, l * B * FC + FIRST)
                sp.wait_ge(fxn_ready, l * B + FIRST)
                sp.wait_ge(fgate_ready, l * B * FC + FIRST)
                sp.wait_ge(fval_ready, l * B * FC + FIRST)
                sp.dma_start(wf[:, F_1:F_2], ffn_w[l, :, F_1:F_2]).then_inc(w1_in, 16)
                sp.wait_ge(w2_done, l * B + FIRST)
                sp.wait_ge(xnew_ready, l * B + FIRST)
                sp.dma_start(wf[:, F_2:WF_N], ffn_w[l, :, F_2:WF_N]).then_inc(w2_in, 16)
            for g in range(4):
                sp.wait_ge(total_ready, g + 1 + FIRST)
                sp.dma_start(out[g * 4:(g + 1) * 4].rearrange("b p t -> p b t"),
                             skip[:, g * 4 * T:(g + 1) * 4 * T].rearrange("p (b t) -> p b t", t=T)).then_inc(out_in, 16)
            sp.wait_ge(out_in, 64)

        @block.tensor
        def _(pe):
            mm = nc.tensor.matmul
            for own in (pos_done, mean_done, var_done, q0_done, k0_done, v0_done, s0_done, t0_done, pv0_done,
                        aot0_done, y0_done, qk_done, v_done, s_done, n_done, pv_done, t_done, aot_done, y_done,
                        fmean_done, fvar_done, w1_done, w2_done):
                pe.sem_inc(own, FIRST)

            def mean(src, e):
                pe.wait_ge(log_ready, e + FIRST)
                mm(FF[:, 0:T], mean_w[:, :], src, start=True, stop=True).then_inc(mean_done, 1)

            def variance(e):
                pe.wait_ge(dsq_ready, e + 1 + FIRST)
                mm(FF[:, 0:T], mean_w[:, :], dsq[:, :], start=True, stop=True).then_inc(var_done, 1)

            def q_project(b, r):
                pe.wait_ge(k0_ready, 2 * b + r + FIRST)
                for i in range(2):
                    c = 2 * r + i
                    last = mm(QK1[:, i * T:(i + 1) * T], hw[:, A_Q + c * P:A_Q + (c + 1) * P], xn[:, :],
                              start=True, stop=True)
                last.then_inc(q0_done, 1)

            def k_project(b, r):
                pe.wait_ge(q0_ready, 2 * b + r + 1 + FIRST)
                for i in range(2):
                    c = 2 * r + i
                    last = mm(QK1[:, i * T:(i + 1) * T], hw[:, A_K + c * P:A_K + (c + 1) * P], xn[:, :],
                              start=True, stop=True)
                last.then_inc(k0_done, 1)

            def prepare():
                pe.wait_ge(setup_ready, 1 + FIRST)
                pe.wait_ge(x0_in, 16)
                mean(slot(stream, 0), 0)
                variance(0)
                pe.wait_ge(hope_in, 32)
                pe.wait_ge(consts_in, 16)
                for c in range(2):
                    last = mm(OO[:, c:c + 1], cst[0:64, C_POS + c * P:C_POS + (c + 1) * P],
                              hv[0:64, V_POS:V_POS + 1], start=True, stop=True)
                last.then_inc(pos_done, 1)
                pe.wait_ge(hbias_ready, 1 + FIRST)
                pe.wait_ge(ln_ready, 1 + FIRST)
                q_project(0, 0)
                k_project(0, 0)

            def body(b, prev, nxt):
                def scores0(h):
                    c, s = h // HPC0, STRIP * (h % HPC0)
                    sc = (S0, S1)[h % 2]
                    if h in (0, 8):
                        pe.wait_ge(q0_ready, 2 * b + h // 8 + 1 + FIRST)
                        pe.wait_ge(k0_ready, 2 * b + h // 8 + 1 + FIRST)
                    if prev or h >= 2:
                        pe.wait_ge(p0_ready, b * H + h - 1 + FIRST)
                    if h < 8:
                        if not prev:
                            pe.wait_ge(bias0_ready, h + 1 + FIRST)
                            pe.wait_ge(casts_ready, 4 + FIRST)
                        ts = slice(h * S0W, (h + 1) * S0W)
                        mm(sc[:, 0:S0W], identr[:, :], tr[:, ts], start=True, stop=False)
                        mm(sc[:, 0:S0W], identr[:, :], th[:, ts], start=False, stop=False)
                    else:
                        mm(sc[:, 0:S0W], identb[:, :], causalb[:, :], start=True, stop=False)
                    mm(sc[:, 0:P], qh[s:s + STRIP, c, 0:P], kh[s:s + STRIP, c, 0:P], start=False, stop=False)
                    mm(sc[:, P:S0W], qh[s:s + STRIP, c, P:T], kh[s:s + STRIP, c, :],
                       start=False, stop=True).then_inc(s0_done, 1)

                for h in range(H):
                    scores0(h)
                    if prev or h >= 1:
                        transposes0(b, h - 1, prev)
                    if prev or h >= 2:
                        values0(b, h - 2)
                    if h == SLOT_V:
                        if prev:
                            pe.wait_ge(aot0_ready, b - 1 + FIRST)
                        for t in range(TQ):
                            last = mm(NV[:, t * P:(t + 1) * P], xn[:, t * P:(t + 1) * P], hw[:, A_V:A_V + P],
                                      start=True, stop=True)
                        last.then_inc(v0_done, 1)
                    if h == SLOT_Q1:
                        q_project(b, 1)
                    if prev and h == SLOT_OUT:
                        pe.wait_ge(v0_ready, b + 1 + FIRST)
                        output(b - 1)
                    if h == SLOT_K1:
                        k_project(b, 1)
                    if prev and h == SLOT_Y:
                        project(b - 1, 2 * b)
                    if prev and h == SLOT_MEAN2:
                        pe.wait_ge(x1_ready, b + FIRST)
                        mean(slot(skip, b - 1), 2 * b)
                    if prev and h == SLOT_VAR2:
                        variance(2 * b)
                    if nxt and h == SLOT_MEAN1:
                        if not prev:
                            pe.wait_ge(x_in, 48)
                        mean(slot(stream, b + 1), 2 * b + 1)
                    if nxt and h == SLOT_VAR1:
                        variance(2 * b + 1)
                    if nxt and h == SLOT_Q0:
                        pe.wait_ge(ln_ready, 2 * b + 2 + FIRST)
                        q_project(b + 1, 0)
                    if nxt and h == SLOT_K0:
                        k_project(b + 1, 0)

            def transposes0(b, h, prev):
                tb = (TT, QK0)[h % 2]
                pe.wait_ge(p0_ready, b * H + h + 1 + FIRST)
                if prev or h >= 2:
                    pe.wait_ge(pt0_ready, b * H + h - 1 + FIRST)
                for i in range(3):
                    last = nc.tensor.transpose(tb[:, i * P:(i + 1) * P], prob0[:, h % 2, i * P:(i + 1) * P], ident)
                last.then_inc(t0_done, 1)

            def values0(b, h):
                if h == 0:
                    pe.wait_ge(v0_ready, b + 1 + FIRST)
                    pe.wait_ge(ao0_ready, b + FIRST)
                pe.wait_ge(pt0_ready, b * H + h + 1 + FIRST)
                o = OO[:, 0:TQ * H * (HD0 + 1)].rearrange("p (t h e) -> p t h e", t=TQ, h=H)
                hh = h % H
                mm(o[:, 0, hh, :], pt0[:, h % 2, 0:P], v0[:, 0, hh, :], start=True, stop=True)
                mm(o[:, 1, hh, :], pt0[:, h % 2, P:2 * P], v0[:, 0, hh, :], start=True, stop=False)
                mm(o[:, 1, hh, :], pt0[:, h % 2, 2 * P:3 * P], v0[:, 1, hh, :], start=False, stop=True)\
                    .then_inc(pv0_done, 1)

            def output(b):
                pe.wait_ge(ao0_ready, b + 1 + FIRST)
                for t in range(TQ):
                    last = nc.tensor.transpose(NV[:, t * P:(t + 1) * P], ao0[:, t, :], ident)
                last.then_inc(aot0_done, 1)

            def project(b, e):
                pe.wait_ge(log_ready, e + FIRST)
                pe.wait_ge(aot0_ready, b + 1 + FIRST)
                mm(FF[:, 0:T], hw[:, A_P:A_P + P], aot0[:, :], start=True, stop=True).then_inc(y0_done, 1)

            def finish():
                transposes0(B, -1, True)
                values0(B, -2)
                values0(B, -1)
                output(B - 1)
                project(B - 1, 2 * B - 1)
                pe.wait_ge(x1_ready, B + FIRST)
                mean(slot(skip, B - 1), 2 * B - 1)
                variance(2 * B - 1)

            attention0(pe, prepare, body, finish)

            def step(l, n, at, p, k0, k1, k2, role, odd):
                G = n * NCH + p
                if k0:
                    w, qk = p * 2 * P, (QK0, QK1)[p % 2]
                    if role == "first":
                        pe.wait_ge(split_ready, l * NCH + p + 1 + FIRST)
                    if p == 0:
                        pe.wait_ge(xs_ready, n + 1 + FIRST)
                    pe.wait_ge(sq_ready, G - 1 + FIRST)
                    for i in range(2):
                        c = w + i * P
                        o = qk[:, i * T:(i + 1) * T]
                        mm(o, wr[:, c:c + P], xh[:, odd, :], start=True, stop=False)
                        mm(o, wh[:, c:c + P], xr[:, odd, :], start=False, stop=False)
                        last = mm(o, wh[:, c:c + P], xh[:, odd, :], start=False, stop=True)
                    last.then_inc(qk_done, 1)
                    pe.wait_ge(guard_ready, G + FIRST)
                    for t in range(TQ):
                        last = mm(NV[:, t * P:(t + 1) * P], xs[:, odd, t * P:(t + 1) * P], wv[:, p * P:(p + 1) * P],
                                  start=True, stop=True)
                    last.then_inc(v_done, 1)
                if k2 and p == 4:
                    pe.wait_ge(fh_ready, n - 1 + FIRST)
                    for j in range(FC):
                        last = mm(FF[:, 0:T], wf[:, F_2 + j * P:F_2 + (j + 1) * P], fh[:, j, :],
                                  start=(j == 0), stop=(j == FC - 1))
                    last.then_inc(w2_done, 1)
                if present(p, 4, k0, k1):
                    pe.wait_ge(p_ready, G - 3 + FIRST)
                    if present(p, 6, k0, k1):
                        pe.wait_ge(aot_ready, G - 5 + FIRST)
                    for t in range(TQ):
                        for i in range(HPC):
                            k = TQ * t + i
                            src = pa[:, p % 2, i, :] if t == 0 else pb[:, p % 2, i, WIN:KB]
                            last = nc.tensor.transpose(TT[:, k * P:(k + 1) * P], src, ident)
                    last.then_inc(t_done, 1)
                if k1 and p == 6:
                    pe.wait_ge(xs2_ready, n + FIRST)
                    mm(FF[:, 0:T], mean_w[:, :], xs2[:, :], start=True, stop=True).then_inc(fmean_done, 1)
                if present(p, 2, k0, k1):
                    par = p % 2
                    pe.wait_ge(p_ready, G - 2 + FIRST)
                    pe.wait_ge(kr_ready, G - 1 + FIRST)
                    for sc in (S0, S1):
                        mm(sc[:, 0:2 * KB], identb[:, :], localb[:, :], start=True, stop=False)
                    for i, sc in enumerate((S0, S1)):
                        f = HD * i
                        mm(sc[:, 0:P], qkr[f:f + HD, par, 0:P], kr[f:f + HD, par, 0:P], start=False, stop=False)
                    for i, sc in enumerate((S0, S1)):
                        f = HD * i
                        last = mm(sc[:, KB:2 * KB], qkr[f:f + HD, par, P:T], kr[f:f + HD, par, P - WIN:T],
                                  start=False, stop=True)
                    last.then_inc(s_done, 1)
                if present(p, 4, k0, k1):
                    par, c = p % 2, (p - 4) % NCH
                    pe.wait_ge(pt_ready, G - 3 + FIRST)
                    pe.wait_ge(ptp_ready, G - 3 + FIRST)
                    pe.wait_ge(ao_ready, G - 4 + FIRST)
                    o = OO[:, 0:4 * (HD + 1)].rearrange("p (k e) -> p k e", e=HD + 1)
                    for i in range(HPC):
                        mm(o[:, HPC + i, :], pt[:, par, (2 + i) * P:(3 + i) * P], vs[:, c, 1, i, :],
                           start=(i == 0), stop=False)
                        mm(o[0:WIN, HPC + i, :], ptp[:, par, i, :], vp[:, c, i, :], start=False, stop=False)
                    for i in range(HPC):
                        last = mm(o[:, i, :], pt[:, par, i * P:(i + 1) * P], vs[:, c, 0, i, :],
                                  start=False, stop=(i == HPC - 1))
                    last.then_inc(pv_done, 1)
                if k1 and p == 5:
                    if role == "second":
                        pe.wait_ge(wo_in, l * 16 + 16)
                    pe.wait_ge(xnew_ready, n - 1 + FIRST)
                    pe.wait_ge(aot_ready, n * NCH + FIRST)
                    for c in range(NCH):
                        last = mm(FF[:, 0:T], wf[:, F_O + c * P:F_O + (c + 1) * P], aot[:, c, :],
                                  start=(c == 0), stop=(c == NCH - 1))
                    last.then_inc(y_done, 1)
                if k1 and p == 6:
                    pe.wait_ge(fdsq_ready, n + FIRST)
                    mm(FF[:, 0:T], mean_w[:, :], dsq[:, :], start=True, stop=True).then_inc(fvar_done, 1)
                if k2 and p < 3:
                    up(n - 2, p)
                if present(p, 5, k0, k1):
                    pe.wait_ge(ao_ready, G - 4 + FIRST)
                    if present(p, 4, k0, k1):
                        pe.wait_ge(pt_ready, G - 3 + FIRST)
                    else:
                        pe.wait_ge(aot_ready, G - 5 + FIRST)
                    for t in range(TQ):
                        last = nc.tensor.transpose(TT[:, t * P:(t + 1) * P], ao[:, (p - 5) % 2, t, :], ident)
                    last.then_inc(aot_done, 1)
                if k0:
                    pe.wait_ge(sq_ready, G + 1 + FIRST)
                    pe.wait_ge(v_ready, G + 1 + FIRST)
                    mm(NV[:, 0:T], blk, sq[:, T:2 * T], start=True, stop=True)
                    for t in range(TQ):
                        last = mm(NV[:, T + 2 * t:T + 2 * t + 2], sq[:, t * P:(t + 1) * P], cst[:, C_BLK:C_BLK + P:HD],
                                  start=True, stop=True)
                    last.then_inc(n_done, 1)
                if role == "second" and p == 7:
                    pe.wait_ge(w1r_ready, l + 1 + FIRST)
                    pe.wait_ge(w2_in, l * 16 + 16)

            def up(m, j):
                pe.wait_ge(nr_ready, m + 1 + FIRST)
                if j:
                    pe.wait_ge(fval_ready, m * FC + j + FIRST)
                for i in range(2):
                    c = (2 * j + i) * P
                    o = FF[:, i * T:(i + 1) * T]
                    mm(o, w1r[:, c:c + P], nh[:, :], start=True, stop=False)
                    mm(o, w1h[:, c:c + P], nr[:, :], start=False, stop=False)
                    last = mm(o, w1h[:, c:c + P], nh[:, :], start=False, stop=True)
                last.then_inc(w1_done, 1)

            pipeline(pe, step)

        @block.vector
        def _(dve):
            v = nc.vector
            for own in (setup_ready, casts_ready, hbias_ready, dev_ready, ln_ready, k0_ready, v0_ready,
                        max0_ready, pt0_ready, rec0_ready, ao0_ready, x1_ready, tables_ready, split_ready, high_ready,
                        shift_ready, xh_ready, xs_ready, v_ready,
                        qkc_ready, qkx_ready, guard_ready, max_ready, nb_ready, ptp_ready, rec_ready, ao_ready,
                        xm_ready, xs2_ready, fdev_ready, fnorm_ready, fxn_ready, nh_ready,
                        nr_ready, w1h_ready, w1r_ready, fval_ready, fh_ready,
                        xnew_ready, total_ready):
                dve.sem_inc(own, FIRST)

            def centre(src, e):
                dve.wait_ge(mean_done, e + 1 + FIRST)
                dve.wait_ge(ln_ready, e + FIRST)
                v.tensor_tensor(dev[:, :], src, FF[:, 0:T], ALU.subtract).then_inc(dev_ready, 1)

            def scale(dst, e):
                dve.wait_ge(rstd_ready, e + 1 + FIRST)
                v.tensor_tensor(dst, dev[:, :], rstd[:, :], ALU.mult).then_inc(ln_ready, 1)

            v.memset(mean_w[:, :], 1.0 / D)
            v.memset(eps[:, :], EPS)
            v.memset(v0[:, :, :, :], 1.0)
            v.memset(vs[:, :, :, :, :], 1.0)
            v.memset(vp[:, :, :, :], 1.0)
            v.memset(xs2[:, :], 0.0).then_inc(setup_ready, 1)
            dve.wait_ge(setup_ready, 1 + FIRST)
            centre(slot(stream, 0), 0)
            scale(xn[:, :], 0)
            dve.wait_ge(consts_in, 16)
            v.tensor_copy(identb[:, :], ident).then_inc(casts_ready, 1)
            v.tensor_copy(causalb[:, :], cst[:, C_CAUSAL:C_CAUSAL + S0W]).then_inc(casts_ready, 1)
            v.tensor_copy(localb[:, :], cst[:, C_LOCAL:C_LOCAL + 2 * KB]).then_inc(casts_ready, 1)
            v.tensor_copy(identr[:, :], ident).then_inc(casts_ready, 1)
            dve.wait_ge(hope_in, 32)
            v.tensor_scalar(hbias[:, 0:4], hv[:, V_BQ:V_BQ + 4], HD0 ** -0.5, cst[:, C_ONE:C_ONE + 1],
                            ALU.mult, ALU.add)
            v.tensor_copy(hbias[:, 4:6], hv[:, V_BK:V_BK + 2])
            dve.wait_ge(pos_done, 1 + FIRST)
            v.tensor_tensor(hbias[:, 6:8], OO[:, 0:2], hv[:, V_BK + 2:V_BK + 4], ALU.add).then_inc(hbias_ready, 1)
            dve.wait_ge(hbias_ready, 1 + FIRST)

            def k_evac(b, r):
                dve.wait_ge(k0_done, 2 * b + r + 1 + FIRST)
                for i in range(2):
                    c = 2 * r + i
                    last = v.tensor_scalar(kh[:, c, :], QK1[:, i * T:(i + 1) * T], hbias[:, 4 + c:5 + c], None, ALU.add)
                last.then_inc(k0_ready, 1)

            def prepare():
                k_evac(0, 0)

            def body(b, prev, nxt):
                for h in range(H):
                    sc = (S0, S1)[h % 2]
                    dve.wait_ge(s0_done, b * H + h + 1 + FIRST)
                    v.tensor_reduce(nmax0[:, h, 0:1], sc[:, 0:P], AX, ALU.max, negate=True)
                    v.tensor_reduce(nmax0[:, h, 1:2], sc[:, P:S0W], AX, ALU.max, negate=True)\
                        .then_inc(max0_ready, 1)
                    if prev or h >= 1:
                        pt_evac(b, h - 1, prev)
                    if h == SLOT_Q1:
                        if prev:
                            normalise(b - 1)
                        dve.wait_ge(v0_done, b + 1 + FIRST)
                        v.tensor_copy(v0[:, :, :, 0:HD0], NV[:, 0:T].rearrange("p (t h e) -> p t h e", t=TQ, h=H))\
                            .then_inc(v0_ready, 1)
                    if h == SLOT_K1:
                        k_evac(b, 1)
                    if prev and h == SLOT_Y:
                        add_x(b - 1)
                    if prev and h == SLOT_MEAN2:
                        centre(slot(skip, b - 1), 2 * b)
                    if prev and h == SLOT_VAR2 + 1:
                        scale(slot(stream, b - 1), 2 * b)
                    if nxt and h == SLOT_MEAN1:
                        centre(slot(stream, b + 1), 2 * b + 1)
                    if nxt and h == SLOT_VAR1 + 1:
                        scale(xn[:, :], 2 * b + 1)
                    if nxt and h == SLOT_K0:
                        k_evac(b + 1, 0)

            def pt_evac(b, h, prev):
                dve.wait_ge(t0_done, b * H + h + 1 + FIRST)
                if prev or h >= 2:
                    dve.wait_ge(pv0_done, b * H + h - 1 + FIRST)
                v.tensor_copy(pt0[:, h % 2, :], (TT, QK0)[h % 2][:, 0:S0W]).then_inc(pt0_ready, 1)

            def normalise(b):
                dve.wait_ge(pv0_done, b * H + H + FIRST)
                dve.wait_ge(aot0_done, b + FIRST)
                o = OO[:, 0:TQ * H * (HD0 + 1)].rearrange("p (k e) -> p k e", e=HD0 + 1)
                v.reciprocal(rec0[:, :], o[:, :, HD0]).then_inc(rec0_ready, 1)
                dve.wait_ge(rec0_ready, b + 1 + FIRST)
                v.tensor_tensor(ao0[:, :, :].rearrange("p t (h e) -> p (t h) e", e=HD0), o[:, :, 0:HD0],
                                rec0[:, :].unsqueeze(2).to_broadcast([P, TQ * H, HD0]), ALU.mult)\
                    .then_inc(ao0_ready, 1)

            def add_x(b):
                dve.wait_ge(y0_done, b + 1 + FIRST)
                v.scalar_tensor_tensor(slot(skip, b), FF[:, 0:T], hv[:, V_BP:V_BP + 1], slot(stream, b),
                                       ALU.add, ALU.add).then_inc(x1_ready, 1)

            def finish():
                pt_evac(B, -1, True)
                normalise(B - 1)
                add_x(B - 1)
                centre(slot(skip, B - 1), 2 * B - 1)
                scale(slot(stream, B - 1), 2 * B - 1)

            attention0(dve, prepare, body, finish)

            def split(k, c):
                ws, wq = slice(c * 2 * P, (c + 1) * 2 * P), slice(c * WCH, c * WCH + 2 * P)
                v.tensor_copy(wh[:, ws], wa[:, wq]).then_inc(high_ready, 1)
                v.tensor_copy(wv[:, c * P:(c + 1) * P], wa[:, c * WCH + 2 * P:(c + 1) * WCH])
                dve.wait_ge(high_ready, k + 1 + FIRST)
                v.tensor_tensor(wr[:, ws], wa[:, wq], wh[:, ws], ALU.subtract).then_inc(split_ready, 1)

            def shift(n, par, src):
                v.tensor_copy(xs[0:HD, par, :], src[0:HD, :])
                v.tensor_copy(xs[HD:P, par, 1:T], src[HD:P, 0:T - 1]).then_inc(shift_ready, 1)
                dve.wait_ge(shift_ready, n + 2 + FIRST)
                v.tensor_copy(xh[:, par, :], xs[:, par, :]).then_inc(xh_ready, 1)
                dve.wait_ge(xh_ready, n + 1 + FIRST)
                v.tensor_tensor(xr[:, par, :], xs[:, par, :], xh[:, par, :], ALU.subtract).then_inc(xs_ready, 1)

            def step(l, n, at, p, k0, k1, k2, role, odd):
                G = n * NCH + p
                if role == "first" and p == 0:
                    dve.wait_ge(wa_in, l * 16 + 16)
                    sc = NCH * WCH
                    for i in range(2):
                        last = v.tensor_scalar(cosw[:, i * T:(i + 1) * T], cst[:, C_COS + i * T:C_COS + (i + 1) * T],
                                               wa[:, sc + 2 * i:sc + 2 * i + 1], None, ALU.mult)
                    last.then_inc(tables_ready, 1)
                    dve.wait_ge(tables_ready, l + 1 + FIRST)
                if present(p, 1, k0, k1):
                    dve.wait_ge(n_done, G + FIRST)
                    dve.wait_ge(log2_ready, G - 1 + FIRST)
                    v.tensor_scalar(ng[:, :], NV[:, 0:T + 4], NORM_GUARD, None, ALU.max).then_inc(guard_ready, 1)
                if k2 and p == 4:
                    dve.wait_ge(fact_ready, n - 1 + FIRST)
                    dve.wait_ge(fval_ready, (n - 1) * FC + FIRST)
                    dve.wait_ge(w2_done, n - 2 + FIRST)
                    v.tensor_tensor(fh[:, :, :], fval[:, :, :], fact[:, :, :], ALU.mult).then_inc(fh_ready, 1)
                if k0:
                    dve.wait_ge(qk_done, G + 1 + FIRST)
                    if p >= 2 or k1:
                        dve.wait_ge(qkr_ready, G - 1 + FIRST)
                    qk = (QK0, QK1)[p % 2]
                    v.tensor_tensor(qkc[:, p % 2, :], qk[:, :], cosw[:, :], ALU.mult).then_inc(qkc_ready, 1)
                    v.stream_shuffle(qkx[:, p % 2, :], qk[:, :], SWAP).then_inc(qkx_ready, 1)
                if present(p, 4, k0, k1):
                    dve.wait_ge(p_ready, G - 3 + FIRST)
                    if present(p, 6, k0, k1):
                        dve.wait_ge(pv_done, G - 5 + FIRST)
                    v.transpose(ptp[:, p % 2, :, :], pb[0:WIN, p % 2, :, 0:WIN]).then_inc(ptp_ready, 1)
                if k2 and 1 <= p <= 3:
                    value(n - 2, p - 1)
                if k2 and p == 5:
                    dve.wait_ge(w2_done, n - 1 + FIRST)
                    v.scalar_tensor_tensor(slot(stream, at[2]), FF[:, 0:T], wf[:, F_B2:F_B2 + 1], xm[:, :],
                                           ALU.add, ALU.add).then_inc(xnew_ready, 1)
                if k0:
                    dve.wait_ge(v_done, G + 1 + FIRST)
                    nv = NV[:, 0:T].rearrange("p (t i e) -> p t i e", t=TQ, i=HPC)
                    v.tensor_copy(vs[:, p, :, :, 0:HD], nv)
                    v.tensor_copy(vp[:, p, :, 0:HD], nv[P - WIN:P, 0, :, :]).then_inc(v_ready, 1)
                    if p == 5 and at[3] is not None:
                        shift(n + 1, 1 - odd, slot(stream, at[3]))
                    if role == "first" and not k1 and p + 1 < NCH:
                        split(p + 1, p + 1)
                    if role == "last" and at[3] is not None:
                        if p == 0:
                            dve.wait_ge(wa_in, l * 16 + 32)
                        split((l + 1) * NCH + p, p)
                if k1 and p == 6:
                    dve.wait_ge(fmean_done, n + FIRST)
                    v.tensor_tensor(dev[:, :], xs2[:, :], FF[:, 0:T], ALU.subtract).then_inc(fdev_ready, 1)
                if k2 and p == 0:
                    dve.wait_ge(fnorm_ready, n - 1 + FIRST)
                    v.tensor_scalar(xn[:, :], dev[:, :], wf[:, F_B:F_B + 1], None, ALU.add)\
                        .then_inc(fxn_ready, 1)
                    dve.wait_ge(fxn_ready, n - 1 + FIRST)
                    v.tensor_copy(nh[:, :], xn[:, :]).then_inc(nh_ready, 1)
                    dve.wait_ge(nh_ready, n - 1 + FIRST)
                    v.tensor_tensor(nr[:, :], xn[:, :], nh[:, :], ALU.subtract).then_inc(nr_ready, 1)
                if present(p, 2, k0, k1):
                    par = p % 2
                    dve.wait_ge(s_done, G - 1 + FIRST)
                    dve.wait_ge(nb_ready, G - 2 + FIRST)
                    v.tensor_reduce(nm[:, 0:2], S0[:, 0:2 * KB].rearrange("p (i j) -> p i j", j=KB), AX, ALU.max,
                                    negate=True)
                    v.tensor_reduce(nm[:, 2:4], S1[:, 0:2 * KB].rearrange("p (i j) -> p i j", j=KB), AX, ALU.max,
                                    negate=True).then_inc(max_ready, 1)
                    dve.wait_ge(max_ready, G - 1 + FIRST)
                    dve.wait_ge(rn_ready, G - 1 + FIRST)
                    if present(p, 4, k0, k1):
                        dve.wait_ge(p_ready, G - 3 + FIRST)
                    v.tensor_tensor(nb[:, par, :].rearrange("p (i t) -> p i t", t=TQ),
                                    nm[:, :].rearrange("p (i t) -> p i t", t=TQ),
                                    rn[:, par, T:T + 4].rearrange("p (t i) -> p i t", i=HPC), ALU.mult)\
                        .then_inc(nb_ready, 1)
                if role == "second" and p == 5:
                    dve.wait_ge(w1_in, l * 16 + 16)
                    v.tensor_copy(w1h[:, :], wf[:, F_1:F_G]).then_inc(w1h_ready, 1)
                    dve.wait_ge(w1h_ready, l + 1 + FIRST)
                    v.tensor_tensor(w1r[:, :], wf[:, F_1:F_G], w1h[:, :], ALU.subtract).then_inc(w1r_ready, 1)
                if k1 and p == 7:
                    dve.wait_ge(frstd_ready, n + FIRST)
                    v.scalar_tensor_tensor(dev[:, :], dev[:, :], wf[:, F_G:F_G + 1], rstd[:, :], ALU.mult, ALU.mult)\
                        .then_inc(fnorm_ready, 1)
                if present(p, 4, k0, k1):
                    dve.wait_ge(pv_done, G - 3 + FIRST)
                    if present(p, 6, k0, k1):
                        dve.wait_ge(aot_done, G - 5 + FIRST)
                    o = OO[:, 0:4 * (HD + 1)].rearrange("p (k e) -> p k e", e=HD + 1)
                    dve.wait_ge(ao_ready, G - 4 + FIRST)
                    v.reciprocal(rec[:, :], o[:, :, HD]).then_inc(rec_ready, 1)
                    dve.wait_ge(rec_ready, G - 3 + FIRST)
                    v.tensor_tensor(ao[:, p % 2, :, :].rearrange("p t (i e) -> p (t i) e", e=HD), o[:, :, 0:HD],
                                    rec[:, :].unsqueeze(2).to_broadcast([P, 4, HD]), ALU.mult)\
                        .then_inc(ao_ready, 1)
                if k1 and p == 5:
                    dve.wait_ge(y_done, n + FIRST)
                    dve.wait_ge(xnew_ready, n - 1 + FIRST)
                    v.tensor_tensor(xm[:, :], FF[:, 0:T], slot(stream, at[1]), ALU.add).then_inc(xm_ready, 1)
                    dve.wait_ge(xm_ready, n + FIRST)
                    v.tensor_copy(xs2[0:HD, :], xm[0:HD, :])
                    v.tensor_copy(xs2[HD:P, 1:T], xm[HD:P, 0:T - 1]).then_inc(xs2_ready, 1)
                if role == "second" and p == 7:
                    dve.wait_ge(w2_in, l * 16 + 16)

            def value(m, j):
                dve.wait_ge(fgate_ready, m * FC + j + 1 + FIRST)
                if j == 0:
                    dve.wait_ge(fh_ready, m + FIRST)
                v.tensor_scalar(fval[:, j, :], FF[:, 0:T], wf[:, F_B1 + 2 * j:F_B1 + 2 * j + 1], None, ALU.add)\
                    .then_inc(fval_ready, 1)

            dve.wait_ge(ln_ready, 2 * B + FIRST)
            v.memset(xs[:, :, :], 0.0).then_inc(shift_ready, 1)
            dve.wait_ge(shift_ready, 1 + FIRST)
            dve.wait_ge(wa_in, 16)
            split(0, 0)
            shift(0, 0, slot(stream, 0))
            pipeline(dve, step)
            dve.wait_ge(xnew_ready, L * B + FIRST)
            for g in range(4):
                w = B * T // 4
                v.tensor_tensor(skip[:, g * w:(g + 1) * w], stream[:, g * w:(g + 1) * w], skip[:, g * w:(g + 1) * w],
                                ALU.add)\
                    .then_inc(total_ready, 1)

        @block.scalar
        def _(act):
            a = nc.scalar.activation
            for own in (dsq_ready, log_ready, rstd_ready, q0_ready, p0_ready, aot0_ready, sq_ready, log2_ready,
                        rn_ready, p_ready, pt_ready, aot_ready, fdsq_ready, flog_ready, frstd_ready, fgate_ready,
                        fact_ready):
                act.sem_inc(own, FIRST)
            nc.scalar.preload_act_table_set("natural_log_exp_and_others")
            act.wait_ge(setup_ready, 1 + FIRST)

            def squares(e):
                act.wait_ge(dev_ready, e + 1 + FIRST)
                a(dsq[:, :], dev[:, :], ACT.Square).then_inc(dsq_ready, 1)

            def deviation(e):
                act.wait_ge(var_done, e + 1 + FIRST)
                a(logv[:, :], FF[:, 0:T], ACT.Ln, bias=eps[:, 0:1]).then_inc(log_ready, 1)
                act.wait_ge(log_ready, e + 1 + FIRST)
                a(rstd[:, :], logv[:, :], ACT.Exp, scale=-0.5).then_inc(rstd_ready, 1)

            def q_evac(b, r):
                act.wait_ge(q0_done, 2 * b + r + 1 + FIRST)
                for i in range(2):
                    c = 2 * r + i
                    last = a(qh[:, c, :], QK1[:, i * T:(i + 1) * T], ACT.Identity, bias=hbias[:, c:c + 1],
                             scale=HD0 ** -0.5)
                last.then_inc(q0_ready, 1)

            def prepare():
                squares(0)
                deviation(0)
                act.wait_ge(hbias_ready, 1 + FIRST)
                q_evac(0, 0)

            def body(b, prev, nxt):
                for h in range(H):
                    sc = (S0, S1)[h % 2]
                    act.wait_ge(max0_ready, b * H + h + 1 + FIRST)
                    if prev or h >= 2:
                        act.wait_ge(t0_done, b * H + h - 1 + FIRST)
                    a(prob0[:, h % 2, 0:P], sc[:, 0:P], ACT.Exp, bias=nmax0[:, h, 0:1])
                    a(prob0[:, h % 2, P:S0W], sc[:, P:S0W], ACT.Exp, bias=nmax0[:, h, 1:2]).then_inc(p0_ready, 1)
                    if h == SLOT_Q1:
                        q_evac(b, 1)
                    if prev and h == SLOT_OUT:
                        out_evac(b - 1)
                    if prev and h == SLOT_MEAN2:
                        squares(2 * b)
                    if prev and h == SLOT_VAR2:
                        deviation(2 * b)
                    if nxt and h == SLOT_MEAN1:
                        squares(2 * b + 1)
                    if nxt and h == SLOT_VAR1:
                        deviation(2 * b + 1)
                    if nxt and h == SLOT_Q0:
                        q_evac(b + 1, 0)

            def out_evac(b):
                act.wait_ge(aot0_done, b + 1 + FIRST)
                a(aot0[:, :], NV[:, 0:T], ACT.Identity, bias=hv[:, V_BV:V_BV + 1]).then_inc(aot0_ready, 1)

            def finish():
                out_evac(B - 1)
                squares(2 * B - 1)
                deviation(2 * B - 1)

            attention0(act, prepare, body, finish)

            def step(l, n, at, p, k0, k1, k2, role, odd):
                G = n * NCH + p
                if present(p, 1, k0, k1):
                    act.wait_ge(guard_ready, G + FIRST)
                    act.wait_ge(rn_ready, G - 1 + FIRST)
                    a(lg[:, :], ng[:, :], ACT.Ln).then_inc(log2_ready, 1)
                    act.wait_ge(log2_ready, G + FIRST)
                    if present(p, 3, k0, k1):
                        act.wait_ge(kr_ready, G - 2 + FIRST)
                        act.wait_ge(p_ready, G - 2 + FIRST)
                    a(rn[:, (p - 1) % 2, :], lg[:, :], ACT.Exp, scale=-0.5).then_inc(rn_ready, 1)
                if present(p, 4, k0, k1):
                    act.wait_ge(t_done, G - 3 + FIRST)
                    if present(p, 6, k0, k1):
                        act.wait_ge(pv_done, G - 5 + FIRST)
                    a(pt[:, p % 2, :], TT[:, :], ACT.Copy).then_inc(pt_ready, 1)
                if k1 and p == 7:
                    act.wait_ge(fvar_done, n + FIRST)
                    a(logv[:, :], FF[:, 0:T], ACT.Ln, bias=eps[:, 0:1]).then_inc(flog_ready, 1)
                    act.wait_ge(flog_ready, n + FIRST)
                    a(rstd[:, :], logv[:, :], ACT.Exp, scale=-0.5).then_inc(frstd_ready, 1)
                if k2 and p == 3:
                    nc.scalar.preload_act_table_set("gelu_and_others")
                if k0:
                    act.wait_ge(qkx_ready, G + 1 + FIRST)
                    act.wait_ge(n_done, G + FIRST)
                    a(sq[:, :], (QK0, QK1)[p % 2][:, :], ACT.Square).then_inc(sq_ready, 1)
                if k2 and p == 3:
                    act.wait_ge(fgate_ready, (n - 1) * FC + FIRST)
                    act.wait_ge(fh_ready, n - 2 + FIRST)
                    a(fact[:, :, :], fgate[:, :, :], ACT.Gelu).then_inc(fact_ready, 1)
                if k2 and p == 3:
                    nc.scalar.preload_act_table_set("natural_log_exp_and_others")
                if k1 and p == 6:
                    act.wait_ge(fdev_ready, n + FIRST)
                    a(dsq[:, :], dev[:, :], ACT.Square).then_inc(fdsq_ready, 1)
                if present(p, 2, k0, k1):
                    par = p % 2
                    act.wait_ge(nb_ready, G - 1 + FIRST)
                    if present(p, 4, k0, k1):
                        act.wait_ge(t_done, G - 3 + FIRST)
                        act.wait_ge(ptp_ready, G - 3 + FIRST)
                    for i, sc in enumerate((S0, S1)):
                        k, r = TQ * i, T + i
                        a(pa[:, par, i, :], sc[:, 0:P], ACT.Exp, bias=nb[:, par, k:k + 1],
                          scale=rn[:, par, r:r + 1])
                        k, r = k + 1, r + HPC
                        last = a(pb[:, par, i, :], sc[:, KB:2 * KB], ACT.Exp, bias=nb[:, par, k:k + 1],
                                 scale=rn[:, par, r:r + 1])
                    last.then_inc(p_ready, 1)
                if k2 and p < 3:
                    gate(n - 2, p)
                if role == "second" and p == 7:
                    act.wait_ge(w1_in, l * 16 + 16)
                if present(p, 5, k0, k1):
                    c = (p - 5) % NCH
                    act.wait_ge(aot_done, G - 4 + FIRST)
                    if c == 0 and k1:
                        act.wait_ge(y_done, n + FIRST)
                    a(aot[:, c, :], TT[:, 0:T], ACT.Copy).then_inc(aot_ready, 1)

            def gate(m, j):
                act.wait_ge(w1_done, m * FC + j + 1 + FIRST)
                if j == 0:
                    act.wait_ge(fact_ready, m + FIRST)
                b1 = F_B1 + 2 * j + 1
                a(fgate[:, j, :], FF[:, T:2 * T], ACT.Identity, bias=wf[:, b1:b1 + 1]).then_inc(fgate_ready, 1)

            pipeline(act, step)

        @block.gpsimd
        def _(pool):
            g = nc.gpsimd
            for own in (high0_ready, bias0_ready, qks_ready, qkr_ready, kr_ready, sinw_ready):
                pool.sem_inc(own, FIRST)

            def step(l, n, at, p, k0, k1, k2, role, odd):
                G = n * NCH + p
                if role == "first" and p == 0:
                    pool.wait_ge(wa_in, l * 16 + 16)
                    sc = NCH * WCH
                    for i in range(2):
                        last = g.tensor_tensor(sinw[:, i * T:(i + 1) * T], cst[:, C_SIN + i * T:C_SIN + (i + 1) * T],
                                               wa[:, sc + 2 * i + 1:sc + 2 * i + 2].to_broadcast([P, T]), ALU.mult)
                    last.then_inc(sinw_ready, 1)
                    pool.wait_ge(sinw_ready, l + 1 + FIRST)
                if present(p, 1, k0, k1):
                    par = (p - 1) % 2
                    pool.wait_ge(qkr_ready, G + FIRST)
                    pool.wait_ge(rn_ready, G + FIRST)
                    if present(p, 3, k0, k1):
                        pool.wait_ge(s_done, G - 2 + FIRST)
                    g.tensor_tensor(kr[:, par, :], qkr[:, par, T:2 * T], rn[:, par, 0:T], ALU.mult)\
                        .then_inc(kr_ready, 1)
                if k0:
                    par = p % 2
                    pool.wait_ge(qkx_ready, G + 1 + FIRST)
                    g.tensor_tensor(qks[:, par, :], qkx[:, par, :], sinw[:, :], ALU.mult).then_inc(qks_ready, 1)
                    pool.wait_ge(qks_ready, G + 1 + FIRST)
                    if p >= 2 or k1:
                        pool.wait_ge(s_done, G - 1 + FIRST)
                    g.tensor_tensor(qkr[:, par, :], qkc[:, par, :], qks[:, par, :], ALU.add).then_inc(qkr_ready, 1)

            pool.wait_ge(toep_in, 16)
            for h in range(8):
                ts = slice(h * S0W, (h + 1) * S0W)
                g.tensor_copy(th[:, ts], toep[:, ts]).then_inc(high0_ready, 1)
                pool.wait_ge(high0_ready, h + 1 + FIRST)
                g.tensor_tensor(tr[:, ts], toep[:, ts], th[:, ts], ALU.subtract).then_inc(bias0_ready, 1)
            pool.wait_ge(ln_ready, 2 * B + FIRST)
            pipeline(pool, step)


def constants():
    c = np.zeros((P, C_N), np.float32)
    c[:, C_ID:C_ID + P] = np.eye(P, dtype=np.float32)
    i = np.arange(P)[:, None]
    ch = np.where(i >= np.arange(P)[None], 0.0, MASKED)
    cw = np.where(i + P >= np.arange(T)[None], 0.0, MASKED)
    c[:, C_CAUSAL:C_CAUSAL + S0W] = np.concatenate([ch, cw], 1)
    d0 = i - np.arange(P)[None]
    d1 = i + WIN - np.arange(KB)[None]
    m0, m1 = (np.where((d >= 0) & (d <= WIN), 0.0, MASKED) for d in (d0, d1))
    none = np.full((P, KB - P), MASKED)
    c[:, C_LOCAL:C_LOCAL + 2 * KB] = np.concatenate([m0, none, m1], 1)
    half = np.arange(0, HD, 2, dtype=np.float32)
    inv_freq = (np.float32(1.0) / np.float32(10000.0) ** (half / np.float32(HD))).astype(np.float32)
    t = np.arange(T, dtype=np.float32)
    fr = t[:, None] * inv_freq[None]
    fr = np.concatenate([fr, fr], 1)
    base = ((half + np.float32(0.4 * HD)) / np.float32(1.4 * HD)).astype(np.float32)
    scale = base[None].astype(np.float64) ** ((t - T // 2) / np.float32(WIN // 2))[:, None].astype(np.float64)
    scale = np.concatenate([scale, scale], 1)
    cos, sin = np.cos(fr.astype(np.float64)), np.sin(fr.astype(np.float64))
    sign = np.where(np.arange(HD) < HD // 2, -1.0, 1.0)[None]
    for k, sc in enumerate((8.0 * scale, 1.0 / scale)):
        at = C_COS + k * T
        c[:, at:at + T] = np.tile((cos * sc).T[ORDER], (2, 1))
        at = C_SIN + k * T
        c[:, at:at + T] = np.tile((sin * sign * sc).T[ORDER], (2, 1))
    c[:, C_BLK:C_BLK + P] = np.kron(np.eye(2), np.ones((HD, HD)))
    rows = np.arange(HPC0) * STRIP + HD0
    c[rows, C_ONE] = 1.0
    for ck in range(2):
        for s in range(HPC0):
            hh = HPC0 * ck + s
            c[8 * hh:8 * hh + 8, C_POS + ck * P + s * STRIP + HD0] = 1.0
    dim = D // 2
    fq = (1.0 / 1250 ** (np.arange(dim, dtype=np.float64) / dim))[:dim - D // 4].astype(np.float32)
    dd = np.arange(-(T - 1), T, dtype=np.float32)
    th = dd[:, None] * fq[None]
    pv = np.cos(th).astype(np.float32) + np.sin(th).astype(np.float32)
    ph = pv.reshape(2 * T - 1, 8, 4).sum(-1)
    tp = np.zeros((P, 8, S0W), np.float32)
    for h in range(8):
        a0 = np.where(ch == 0, ph[i - np.arange(P)[None] + T - 1, h], MASKED)
        a1 = np.where(cw == 0, ph[i + P - np.arange(T)[None] + T - 1, h], MASKED)
        tp[:, h] = np.concatenate([a0, a1], 1)
    return c, tp.reshape(P, 8 * S0W)


def kernel(**inputs):
    import concourse.bacc as bacc
    from concourse.bass_utils import run_bass_kernel_spmd

    g = {k: np.asarray(v) for k, v in inputs.items()}
    f = np.float32
    consts, toeplitz = constants()
    x = np.ascontiguousarray(g["L0_attn_x"].transpose(0, 2, 1))
    wqkv = g["L0_attn_w_qkv"].reshape(3, NC0, HPC0, HD0, D)
    bqkv = g["L0_attn_b_qkv"].reshape(3, NC0, HPC0, HD0)
    hope_w = np.zeros((P, A_N), f)
    hope_v = np.zeros((P, V_N), f)
    for at, bt, k in ((A_Q, V_BQ, 0), (A_K, V_BK, 1)):
        w = np.zeros((NC0, HPC0, STRIP, D), f)
        w[:, :, :HD0] = wqkv[k]
        hope_w[:, at:at + NC0 * P] = w.reshape(NC0 * P, D).T
        bb = np.zeros((NC0, HPC0, STRIP), f)
        bb[:, :, :HD0] = bqkv[k]
        hope_v[:, bt:bt + NC0] = bb.reshape(NC0, P).T
    hope_w[:, A_V:A_V + D] = g["L0_attn_w_qkv"][2 * D:].T
    hope_w[:, A_P:A_P + D] = g["L0_attn_w_proj"].T
    hope_v[:, V_BV] = g["L0_attn_b_qkv"][2 * D:]
    hope_v[:, V_BP] = g["L0_attn_b_proj"]
    hope_v[:64, V_POS] = g["L0_attn_pos_independent"].reshape(64)
    order = np.array(ORDER)
    partner = (order + HD // 2) % HD
    w = g["L0_ffn_Wqkv"].reshape(L, D, 3, NCH, HPC, HD)
    attn_w = np.zeros((L, P, WA_N), f)
    parts = np.stack([w[:, :, 0][..., order], w[:, :, 1][..., order], w[:, :, 2]], 3)
    attn_w[:, :, :NCH * WCH] = parts.reshape(L, D, NCH * WCH)
    for i, (nm, at) in enumerate((("q", order), ("q", partner), ("k", order), ("k", partner))):
        sc = g[f"L0_ffn_{nm}_scale"][:, at]
        attn_w[:, :HD, NCH * WCH + i] = sc
        attn_w[:, HD:, NCH * WCH + i] = sc
    ffn_w = np.zeros((L, P, WF_N), f)
    ffn_w[:, :, F_O:F_O + NCH * P] = g["L0_ffn_Wo"].reshape(L, NCH, P, D).transpose(0, 2, 1, 3).reshape(L, P, NCH * D)
    w1 = np.zeros((L, D, FC, 2, P), f)
    b1 = np.zeros((L, FC, 2, P), f)
    w2 = np.zeros((L, FC * P, D), f)
    w2[:, :FI] = g["L0_ffn_W2"]
    for j in range(FC):
        e = min(P, FI - j * P)
        for i in range(2):
            at = i * FI + j * P
            w1[:, :, j, i, :e] = g["L0_ffn_W1"][:, :, at:at + e]
            b1[:, j, i, :e] = g["L0_ffn_b1"][:, at:at + e]
    ffn_w[:, :, F_1:F_1 + 2 * FC * P] = w1.reshape(L, D, 2 * FC * P)
    ffn_w[:, :, F_2:F_2 + FC * P] = w2.reshape(L, FC, P, D).transpose(0, 2, 1, 3).reshape(L, P, FC * D)
    ffn_w[:, :, F_G] = g["L0_ffn_ln_g"]
    ffn_w[:, :, F_B] = g["L0_ffn_ln_b"]
    ffn_w[:, :, F_B1:F_B1 + 2 * FC] = b1.reshape(L, 2 * FC, P).transpose(0, 2, 1)
    ffn_w[:, :, F_B2] = g["L0_ffn_b2"]

    nc = bacc.Bacc("TRN2", target_bir_lowering=False, num_devices=1)
    arrays, args = {}, []
    for name, arr in (("x", x), ("consts", consts), ("toeplitz", toeplitz), ("hope_w", hope_w), ("hope_v", hope_v),
                      ("attn_w", attn_w), ("ffn_w", ffn_w)):
        arr = np.ascontiguousarray(arr)
        arrays[f"in_{name}"] = arr
        args.append(nc.dram_tensor(f"in_{name}", arr.shape, mybir.dt.from_np(arr.dtype), kind="ExternalInput").ap())
    args.append(nc.dram_tensor("out_y", (B, D, T), F32, kind="ExternalOutput").ap())
    sequence_kernel(nc, *args)
    r = run_bass_kernel_spmd(nc, [arrays], core_ids=[0])
    return np.ascontiguousarray(r.results[0]["out_y"].transpose(0, 2, 1))
```
